# Optimizing a Trainium2 kernel written in Bass

```python
import numpy as np
import jax
import jax.numpy as jnp

def _softmax(x, axis=-1):
    return jax.nn.softmax(x, axis=axis)

def _gelu(x):
    return jax.nn.gelu(x, approximate=True)

def _silu(x):
    return jax.nn.silu(x)

def _sigmoid(x):
    return jax.nn.sigmoid(x)

def _layernorm(x, axis=-1, eps=1e-05):
    m = jnp.mean(x, axis=axis, keepdims=True)
    v = jnp.var(x, axis=axis, keepdims=True)
    return (x - m) / jnp.sqrt(v + eps)

def _scatter_add(tgt, idx, src, axis=0):
    return tgt.at[idx].add(src)

def _segment_sum(src, seg, n):
    return jax.ops.segment_sum(src, seg, n)
kernel_name = 'mk_adj_preln_d4_adj_r2_61312c'

def setup_inputs(seed: int=0):
    np.random.seed(seed)
    _w = jnp.asarray

    def _rec_inputs():
        import jax
        import jax.numpy as jnp
        _gk = jax.random.key(seed)
        x = 7.22e-05 + 1 * jax.random.normal(jax.random.fold_in(_gk, 1), (8, 1024, 256), jnp.float32)
        _a = jax.random.bernoulli(jax.random.fold_in(_gk, 2), 0.00195312, (8, 1024, 1024))
        _a = jnp.logical_or(_a, jnp.eye(1024, dtype=bool))
        _af = _a.astype(jnp.float32)
        _af = _af * jax.random.uniform(jax.random.fold_in(_gk, 3), (8, 1024, 1024), jnp.float32, 0.05, 1)
        adj = _af
        _nm = jnp.ones((8, 1024), dtype=bool)
        nodemask = jnp.where(_nm, 1.0, 0.0).astype(jnp.float32)
        return (x, adj, nodemask)
    x, adj, nodemask = _rec_inputs()

    def _L0_gnn_setup():
        import jax, jax.numpy as jnp
        import numpy as np
        B, N, IN_DIM, ATT_DIM = (2, 4096, 256, 256)
        key = jax.random.key(seed)
        k1, k2, k3, k4 = jax.random.split(key, 4)
        X = jax.random.normal(k1, (B, N, IN_DIM), dtype=jnp.float32)
        adj = jax.random.uniform(k2, (B, N, N), dtype=jnp.float32)
        mask = jnp.ones((B, N), dtype=jnp.float32)
        Wqk = jax.random.normal(k3, (IN_DIM, 2 * ATT_DIM), dtype=jnp.float32) / np.sqrt(IN_DIM)
        Wv = jax.random.normal(k4, (IN_DIM, IN_DIM), dtype=jnp.float32) / np.sqrt(IN_DIM)
        return {'X': X, 'adj': adj, 'mask': mask, 'Wqk': Wqk, 'Wv': Wv}
    _L0_gnn_all = _L0_gnn_setup()
    _L0_gnn_in = {k: v for k, v in _L0_gnn_all.items() if k in ('Wqk', 'Wv')}
    del _L0_gnn_all

    def _L1_gnn_setup():
        import jax, jax.numpy as jnp
        import numpy as np
        EMBED_DIM = 256
        NUM_HEADS = 8
        HEAD_DIM = EMBED_DIM // NUM_HEADS
        SCALE = HEAD_DIM ** (-0.5)
        B, S = (16, 512)
        key = jax.random.key(seed)
        ks = jax.random.split(key, 12)
        init = lambda k, shape: jax.random.normal(k, shape, dtype=jnp.float32) * EMBED_DIM ** (-0.5)
        return {'x': jax.random.normal(ks[0], (B, S, EMBED_DIM), dtype=jnp.float32), 'adj_matrix': jax.random.uniform(ks[1], (B, S, S), dtype=jnp.float32), 'bond_matrix': jax.random.uniform(ks[2], (B, S, S), dtype=jnp.float32), 'Wq': init(ks[3], (EMBED_DIM, EMBED_DIM)), 'bq': jnp.zeros((EMBED_DIM,), jnp.float32), 'Wk': init(ks[4], (EMBED_DIM, EMBED_DIM)), 'bk': jnp.zeros((EMBED_DIM,), jnp.float32), 'Wv': init(ks[5], (EMBED_DIM, EMBED_DIM)), 'bv': jnp.zeros((EMBED_DIM,), jnp.float32), 'Wo': init(ks[6], (EMBED_DIM, EMBED_DIM)), 'bo': jnp.zeros((EMBED_DIM,), jnp.float32), 'seq_len': S}
    _L1_gnn_all = _L1_gnn_setup()
    _L1_gnn_in = {k: v for k, v in _L1_gnn_all.items() if k in ('Wq', 'bq', 'Wk', 'bk', 'Wv', 'bv', 'Wo', 'bo')}
    del _L1_gnn_all

    def _L2_gnn_setup():
        import jax, jax.numpy as jnp
        import numpy as np
        EPS_LN = 1e-05

        def hypergraph_conv(x, adj, W, b):
            N, C, _ = adj.shape
            H = (adj != 0).astype(x.dtype)
            w = adj.reshape(N, -1)[:, :C]
            xw = jnp.einsum('ncd,hd->nch', x, W)
            Dn = jnp.einsum('nce,ne->nc', H, w)
            Dn = jnp.where(Dn > 0, 1.0 / Dn, 0.0)
            Be = H.sum(axis=1)
            Be = jnp.where(Be > 0, 1.0 / Be, 0.0)
            m = Be[:, :, None] * jnp.einsum('nce,nch->neh', H, xw)
            out = Dn[:, :, None] * jnp.einsum('nce,neh->nch', H, m)
            return out + b

        def layer_norm(x, g, b):
            mu = jnp.mean(x, axis=-1, keepdims=True)
            var = jnp.var(x, axis=-1, keepdims=True)
            return (x - mu) * jax.lax.rsqrt(var + EPS_LN) * g + b
        key = jax.random.key(seed)
        ks = jax.random.split(key, 4)
        N, C, Din, Dh, Dout = (16, 512, 256, 512, 256)
        x = jax.random.normal(ks[0], (N, C, Din), dtype=jnp.float32)
        adj = jax.random.uniform(ks[1], (N, C, C), dtype=jnp.float32, minval=0.1, maxval=1.0)
        W1 = jax.random.normal(ks[2], (Dh, Din), dtype=jnp.float32) * (1.0 / np.sqrt(Din))
        b1 = jnp.zeros((Dh,), dtype=jnp.float32)
        gamma = jnp.ones((Dh,), dtype=jnp.float32)
        beta = jnp.zeros((Dh,), dtype=jnp.float32)
        W2 = jax.random.normal(ks[3], (Dout, Dh), dtype=jnp.float32) * (1.0 / np.sqrt(Dh))
        b2 = jnp.zeros((Dout,), dtype=jnp.float32)
        return {'x': x, 'adj': adj, 'W1': W1, 'b1': b1, 'gamma': gamma, 'beta': beta, 'W2': W2, 'b2': b2}
    _L2_gnn_all = _L2_gnn_setup()
    _L2_gnn_in = {k: v for k, v in _L2_gnn_all.items() if k in ('W1', 'b1', 'gamma', 'beta', 'W2', 'b2')}
    del _L2_gnn_all

    def _L3_gnn_setup():
        import jax, jax.numpy as jnp
        import numpy as np
        B, N, D = (8, 1024, 256)
        key = jax.random.key(seed)
        ks = jax.random.split(key, 8)
        scale = 0.5 / np.sqrt(D)
        x = jax.random.normal(ks[0], (B, N, D), dtype=jnp.float32)
        adj = jax.random.uniform(ks[1], (B, N, N), dtype=jnp.float32)
        Wq_w = jax.random.normal(ks[2], (D, D), dtype=jnp.float32) * scale
        Wk_w = jax.random.normal(ks[3], (D, D), dtype=jnp.float32) * scale
        Wv_w = jax.random.normal(ks[4], (D, D), dtype=jnp.float32) * scale
        Wq_b = jnp.zeros((D,), dtype=jnp.float32)
        Wk_b = jnp.zeros((D,), dtype=jnp.float32)
        Wv_b = jnp.zeros((D,), dtype=jnp.float32)
        return {'x': x, 'adj': adj, 'Wq_w': Wq_w, 'Wq_b': Wq_b, 'Wk_w': Wk_w, 'Wk_b': Wk_b, 'Wv_w': Wv_w, 'Wv_b': Wv_b}
    _L3_gnn_all = _L3_gnn_setup()
    _L3_gnn_in = {k: v for k, v in _L3_gnn_all.items() if k in ('Wq_w', 'Wq_b', 'Wk_w', 'Wk_b', 'Wv_w', 'Wv_b')}
    del _L3_gnn_all
    return {'x': x, 'adj': adj, 'nodemask': nodemask, 'L0_gnn_Wqk': _L0_gnn_in['Wqk'], 'L0_gnn_Wv': _L0_gnn_in['Wv'], 'L1_gnn_Wq': _L1_gnn_in['Wq'], 'L1_gnn_bq': _L1_gnn_in['bq'], 'L1_gnn_Wk': _L1_gnn_in['Wk'], 'L1_gnn_bk': _L1_gnn_in['bk'], 'L1_gnn_Wv': _L1_gnn_in['Wv'], 'L1_gnn_bv': _L1_gnn_in['bv'], 'L1_gnn_Wo': _L1_gnn_in['Wo'], 'L1_gnn_bo': _L1_gnn_in['bo'], 'L2_gnn_W1': _L2_gnn_in['W1'], 'L2_gnn_b1': _L2_gnn_in['b1'], 'L2_gnn_gamma': _L2_gnn_in['gamma'], 'L2_gnn_beta': _L2_gnn_in['beta'], 'L2_gnn_W2': _L2_gnn_in['W2'], 'L2_gnn_b2': _L2_gnn_in['b2'], 'L3_gnn_Wq_w': _L3_gnn_in['Wq_w'], 'L3_gnn_Wq_b': _L3_gnn_in['Wq_b'], 'L3_gnn_Wk_w': _L3_gnn_in['Wk_w'], 'L3_gnn_Wk_b': _L3_gnn_in['Wk_b'], 'L3_gnn_Wv_w': _L3_gnn_in['Wv_w'], 'L3_gnn_Wv_b': _L3_gnn_in['Wv_b']}

def reference(x, adj, nodemask, L0_gnn_Wqk, L0_gnn_Wv, L1_gnn_Wq, L1_gnn_bq, L1_gnn_Wk, L1_gnn_bk, L1_gnn_Wv, L1_gnn_bv, L1_gnn_Wo, L1_gnn_bo, L2_gnn_W1, L2_gnn_b1, L2_gnn_gamma, L2_gnn_beta, L2_gnn_W2, L2_gnn_b2, L3_gnn_Wq_w, L3_gnn_Wq_b, L3_gnn_Wk_w, L3_gnn_Wk_b, L3_gnn_Wv_w, L3_gnn_Wv_b):
    import jax
    import jax.numpy as jnp

    def _L0_gnn_ref(X, adj, mask, Wqk, Wv):
        import jax, jax.numpy as jnp
        import numpy as np
        B, N, IN_DIM, ATT_DIM = (2, 4096, 256, 256)
        qk = X @ Wqk
        q, k = jnp.split(qk, 2, axis=-1)
        v = X @ Wv
        att_dim = q.shape[-1]
        inv_scale = 1.0 / jnp.sqrt(jnp.float32(att_dim))
        k_m = k * mask[:, :, None]
        agg = jnp.einsum('bij,bjd->bid', adj, k_m)
        w = inv_scale * mask * jnp.einsum('bid,bid->bi', q, agg)
        L = jax.nn.softmax(w, axis=1)[:, :, None] * v
        return L

    def _L1_gnn_ref(x, adj_matrix, bond_matrix, Wq, bq, Wk, bk, Wv, bv, Wo, bo, seq_len):
        import jax, jax.numpy as jnp
        import numpy as np
        EMBED_DIM = 256
        NUM_HEADS = 8
        HEAD_DIM = EMBED_DIM // NUM_HEADS
        SCALE = HEAD_DIM ** (-0.5)
        B, S = (16, 512)
        b = x.shape[0]

        def proj(W, bias):
            y = jnp.einsum('bse,fe->bsf', x, W) + bias
            return y.reshape(b, seq_len, NUM_HEADS, HEAD_DIM).transpose(0, 2, 1, 3)
        q, k, v = (proj(Wq, bq), proj(Wk, bk), proj(Wv, bv))
        scores = jnp.einsum('bhqd,bhkd->bhqk', q, k) * SCALE
        mask = (adj_matrix + bond_matrix)[:, None, :, :]
        scores = scores * mask
        attn = jax.nn.softmax(scores, axis=-1)
        ctx = jnp.einsum('bhqk,bhkd->bhqd', attn, v)
        ctx = ctx.transpose(0, 2, 1, 3).reshape(b, seq_len, EMBED_DIM)
        return jnp.einsum('bse,fe->bsf', ctx, Wo) + bo

    def _L2_gnn_ref(x, adj, W1, b1, gamma, beta, W2, b2):
        import jax, jax.numpy as jnp
        import numpy as np
        EPS_LN = 1e-05

        def hypergraph_conv(x, adj, W, b):
            N, C, _ = adj.shape
            H = (adj != 0).astype(x.dtype)
            w = adj.reshape(N, -1)[:, :C]
            xw = jnp.einsum('ncd,hd->nch', x, W)
            Dn = jnp.einsum('nce,ne->nc', H, w)
            Dn = jnp.where(Dn > 0, 1.0 / Dn, 0.0)
            Be = H.sum(axis=1)
            Be = jnp.where(Be > 0, 1.0 / Be, 0.0)
            m = Be[:, :, None] * jnp.einsum('nce,nch->neh', H, xw)
            out = Dn[:, :, None] * jnp.einsum('nce,neh->nch', H, m)
            return out + b

        def layer_norm(x, g, b):
            mu = jnp.mean(x, axis=-1, keepdims=True)
            var = jnp.var(x, axis=-1, keepdims=True)
            return (x - mu) * jax.lax.rsqrt(var + EPS_LN) * g + b
        h = jax.nn.relu(hypergraph_conv(x, adj, W1, b1))
        h = layer_norm(h, gamma, beta)
        y = hypergraph_conv(h, adj, W2, b2)
        return y + x

    def _L3_gnn_ref(x, adj, Wq_w, Wq_b, Wk_w, Wk_b, Wv_w, Wv_b):
        import jax, jax.numpy as jnp
        import numpy as np
        B, N, D = (8, 1024, 256)
        query = jnp.einsum('bnd,od->bno', x, Wq_w) + Wq_b
        keyt = jnp.einsum('bnd,od->bno', x, Wk_w) + Wk_b
        value = jnp.einsum('bnd,od->bno', x, Wv_w) + Wv_b
        weight = jnp.einsum('bqd,bkd->bqk', query, keyt)
        weight = adj * jnp.exp(weight)
        weight = weight / jnp.sum(weight, axis=2, keepdims=True)
        return jnp.einsum('bqk,bkd->bqd', weight, value)
    h = jnp.maximum(_layernorm(x, axis=-1), 0.0)
    x = x + _L0_gnn_ref(h, adj, nodemask, L0_gnn_Wqk, L0_gnn_Wv)
    h = jnp.maximum(_layernorm(x, axis=-1), 0.0)
    x = x + _L1_gnn_ref(h, adj, adj, L1_gnn_Wq, L1_gnn_bq, L1_gnn_Wk, L1_gnn_bk, L1_gnn_Wv, L1_gnn_bv, L1_gnn_Wo, L1_gnn_bo, 1024)
    h = jnp.maximum(_layernorm(x, axis=-1), 0.0)
    x = x + _L2_gnn_ref(h, adj, L2_gnn_W1, L2_gnn_b1, L2_gnn_gamma, L2_gnn_beta, L2_gnn_W2, L2_gnn_b2)
    h = jnp.maximum(_layernorm(x, axis=-1), 0.0)
    x = x + _L3_gnn_ref(h, adj, L3_gnn_Wq_w, L3_gnn_Wq_b, L3_gnn_Wk_w, L3_gnn_Wk_b, L3_gnn_Wv_w, L3_gnn_Wv_b)
    return x

_drawn_inputs = setup_inputs


def setup_inputs(seed=0):
    import zlib

    import numpy as np

    out = dict(_drawn_inputs(seed))
    spreads = {'L1_gnn_bq': (0.0, 0.8),
     'L1_gnn_bk': (0.0, 0.8),
     'L1_gnn_bv': (0.0, 0.1),
     'L1_gnn_bo': (0.0, 0.1),
     'L2_gnn_b1': (0.0, 0.1),
     'L2_gnn_gamma': (1.0, 0.2),
     'L2_gnn_beta': (0.0, 0.1),
     'L2_gnn_b2': (0.0, 0.1),
     'L3_gnn_Wq_b': (0.0, 0.353),
     'L3_gnn_Wk_b': (0.0, 0.8),
     'L3_gnn_Wv_b': (0.0, 0.1)}
    factors = {'L0_gnn_Wqk': 8.0, 'L0_gnn_Wv': 8.0, 'L1_gnn_Wq': 8.0, 'L1_gnn_Wk': 8.0}
    for name, (base, spread) in spreads.items():
        noise = np.random.default_rng([zlib.crc32(name.encode()), seed]).standard_normal(out[name].shape)
        drawn = base * np.exp(spread * noise) if base else spread * noise
        out[name] = jnp.asarray(drawn.astype(out[name].dtype))
    for name, factor in factors.items():
        out[name] = (out[name] * factor).astype(out[name].dtype)
    return out
```

```python
from contextlib import ExitStack

import concourse.bass as bass
from concourse import mybir

F32 = mybir.dt.float32
F32R = mybir.dt.float32r
ALU = mybir.AluOpType
ACT = mybir.ActivationFunctionType
AX = mybir.AxisListType

P = 128
HALF = 512
EPS = 1e-5
LOWEST = -3.0e38
TINY = 1.2e-38


class Signal:

    def __init__(self, sem, per):
        self.sem, self.per = sem, per

    def __call__(self, b, n):
        return self.sem, b * self.per + n


def build_program(nc, x_in, adj_in, mask_in, wqkT0, wv0, w1attn, bq1, bk1, bv1, bo1,
                  w1T, b1, gamma, beta, w2T, b2, w3attn, bq3, bk3, bv3, out):
    B, N, D = x_in.shape
    NT = N // P
    DT = D // P
    NH = N // HALF
    TPH = HALF // P
    HID = w1T.shape[1]
    FT = HID // P
    HEADS = 8
    HD = D // HEADS
    HPG = P // HD
    GROUPS = HEADS // HPG
    UNITS = NT * HEADS
    PTS = 8
    ZS = 3
    SCORE_SCALE = 2.0 * float(HD) ** -0.5
    W_SCALE = 1.0 / float(D) ** 0.5

    ctx = ExitStack()
    with ctx:
        def sb(name, shape, dt=F32, scope=ctx):
            return scope.enter_context(nc.sbuf_tensor(name, shape, dt))

        def signal(name, per):
            return Signal(ctx.enter_context(nc.semaphore(name)), per)

        adjN = sb("adjN", [P, NT, N])
        adjT = sb("adjT", [P, NT, N])
        x = sb("x", [P, NT, D])
        ident = sb("ident", [P, P])
        ones = sb("ones", [P, P])
        W0 = sb("W0", [P, DT, 2 * D])
        Wo1 = sb("Wo1", [P, DT, D])
        bq1c = sb("bq1c", [P, DT])
        bk1c = sb("bk1c", [P, DT])
        bq3c = sb("bq3c", [P, DT])
        bk3c = sb("bk3c", [P, DT])
        gammac = sb("gammac", [P, FT])
        betac = sb("betac", [P, FT])
        bv1B = sb("bv1B", [P, D])
        bo1B = sb("bo1B", [P, D])
        b1B = sb("b1B", [P, HID])
        b2B = sb("b2B", [P, D])
        bv3B = sb("bv3B", [P, D])
        cB = sb("cB", [P, D])
        mhalf = sb("mhalf", [P, NT])
        mask = sb("mask", [P, NT])
        mask16 = sb("mask16", [P, NT])
        stats = sb("stats", [P, NT, 6])
        mv = sb("mv", [P, NT, 2])
        ve = sb("ve", [P, NT])
        rstd = sb("rstd", [P, NT])
        nmr = sb("nmr", [P, NT])
        sw = sb("sw", [P, 4, NT])
        s1 = sb("s1", [P, 8])
        mx = sb("mx", [P, UNITS])
        nm = sb("nm", [P, UNITS])
        sm = sb("sm", [P, UNITS])
        rs = sb("rs", [P, 2, HPG, HD])
        Rs = sb("Rs", [P, P])
        ctxn = sb("ctxn", [P, GROUPS, P])
        dn = sb("dn", [P, 4, NT])
        be = sb("be", [P, 2, NT])
        rden = sb("rden", [P, NT])

        def region(*layouts):
            got = []
            for i, layout in enumerate(layouts):
                with ExitStack() as scope:
                    got.append([sb(n if i == 0 else f"{n}_{i}", s, d, scope) for n, s, d in layout])
            sizes = [sum(_bytes(s) for _, s, _ in layout) for layout in layouts]
            sb(f"region_{layouts[0][0][0]}", [P, max(sizes) // 4])
            return got

        def _bytes(shape):
            n = 4
            for s in shape[1:]:
                n *= s
            return n

        HW = D + 2
        common = [("h", [P, NT, HW], F32), ("hT", [P, DT, N], F32)]
        (a0, a1, a2, a3, asetup) = region(
            common + [("mh", [P, NT, D], F32), ("GV", [P, NT, 2 * D], F32)],
            [("qS", [P, HEADS, N], F32R), ("kS", [P, HEADS, N], F32R)],
            common[:1] + [("HT", [P, NT, N], F32), ("U", [P, NT, D], F32), ("A2T", [P, DT, N], F32)],
            common + [("q3T", [P, DT, N], F32), ("k3T", [P, DT, N], F32), ("v3", [P, NT, HW], F32),
                      ("W3", [P, 3, DT, D], F32)],
            [("wqk0s", [P, 4, D], F32), ("betaB", [P, FT, P], F32)],
        )
        h, hT, mh, GV = a0
        qS, kS = a1
        _, HT, U, A2T = a2
        _, _, q3T, k3T, v3, W3 = a3
        wqk0s, betaB = asetup
        (p1a, p1b, p2, p2d, p3) = region(
            [("khi", [P, GROUPS, N], F32R), ("klo", [P, GROUPS, N], F32R),
             ("qhi", [P, GROUPS, N], F32R), ("qlo", [P, GROUPS, N], F32R), ("room", [P, N], F32),
             ("W1", [P, 3, DT, D], F32)],
            [("PT", [P, PTS, NT, P], F32), ("Z", [P, ZS, N], F32)],
            [("h2", [P, NT, HID], F32), ("h2T", [P, FT, N], F32)],
            [("pad", [P, NT, HID], F32), ("wB", [P, N], F32), ("junk", [P, N], F32)],
            [("P3", [P, NH, NT, HALF], F32), ("E3", [P, 2, HALF], F32)],
        )
        khi, klo, qhi, qlo, _, W1 = p1a
        PT, Z = p1b
        h2, h2T = p2
        _, wB, junk = p2d
        P3, E3 = p3
        (r1, r2, r3) = region(
            [("v", [P, NT, D], F32)],
            [("W1h", [P, DT, HID], F32), ("W2g", [P, FT, D], F32)],
            [("xn", [P, NT, D], F32)],
        )
        (v,), (W1h, W2g), (xn,) = r1, r2, r3
        H = adjN
        Wq1, Wk1, Wv1 = (W1[:, i] for i in range(3))

        ps = ctx.enter_context(nc.psum_tensor("ps", [P, 8, HALF], F32))

        weights_in = signal("weights_in", 0)
        consts_ready = signal("consts_ready", 0)
        beta_bc = signal("beta_bc", 0)
        setup_pe = signal("setup_pe", 0)
        setup_dve = signal("setup_dve", 0)
        waited_dve = signal("waited_dve", 0)
        waited_pool = signal("waited_pool", 0)
        waited_sp = signal("waited_sp", 0)
        adj_in_s = signal("adj_in_s", 16)
        x_in_s = signal("x_in_s", 32)
        out_s = signal("out_s", 16)
        x_free = signal("x_free", 1)
        kS_in = signal("kS_in", 256)
        qS_in = signal("qS_in", 256)
        w2_in = signal("w2_in", 32)
        wB_in = signal("wB_in", 16)
        w3_in = signal("w3_in", 48)
        w1_in = signal("w1_in", 48)
        stat = signal("stat", 5 * NT)
        mvs = signal("mvs", 5 * NT)
        ves = signal("ves", 5)
        rstds = signal("rstds", 5)
        nmrs = signal("nmrs", 5)
        hs = signal("hs", 4 * NT)
        hT_ps = signal("hT_ps", 3 * 2 * DT)
        hTs = signal("hTs", 3 * 2 * DT)
        aT_ps = signal("aT_ps", NT * NH)
        aT_act = signal("aT_act", NT * NH // 2)
        aT_dve = signal("aT_dve", NT * NH // 2)
        gv_ps = signal("gv_ps", NT)
        gvs = signal("gvs", NT)
        mhs = signal("mhs", NT)
        agg_ps = signal("agg_ps", NT)
        wrs = signal("wrs", NT)
        chain = signal("chain", 9)
        wm_bc = signal("wm_bc", 1)
        wmT_ps = signal("wmT_ps", 1)
        nwms = signal("nwms", 1)
        es = signal("es", 1)
        esum_ps = signal("esum_ps", 1)
        x0s = signal("x0s", NT)
        xbo = signal("xbo", 1)
        v_ps = signal("v_ps", NT)
        vs = signal("vs", NT)
        kq_ps = signal("kq_ps", 2 * GROUPS * NH)
        hi_s = signal("hi_s", 2 * GROUPS * NH)
        lo_s = signal("lo_s", 2 * GROUPS * NH)
        S_ps = signal("S_ps", UNITS)
        zs = signal("zs", UNITS)
        nms = signal("nms", UNITS)
        exps = signal("exps", UNITS)
        T_ps = signal("T_ps", 2 * UNITS)
        PT_act = signal("PT_act", UNITS + NT)
        PT_dve = signal("PT_dve", UNITS - NT)
        pv_ps = signal("pv_ps", NT * GROUPS)
        R_ps = signal("R_ps", NT * GROUPS)
        rss = signal("rss", NT * GROUPS)
        Rss = signal("Rss", NT * GROUPS)
        ctxs = signal("ctxs", NT * GROUPS)
        o_ps = signal("o_ps", NT)
        x1s = signal("x1s", NT)
        ones_col = signal("ones_col", 2)
        dns = signal("dns", NT)
        Hs = signal("Hs", NT)
        HTs = signal("HTs", NT)
        w2g_s = signal("w2g_s", FT)
        xh = signal("xh", 1)
        xhb = signal("xhb", 1)
        a1_ps = signal("a1_ps", NT)
        be_a = signal("be_a", NT)
        be_b = signal("be_b", NT)
        Us = signal("Us", NT)
        a2_ps = signal("a2_ps", DT * NH)
        a2s = signal("a2s", DT * NH)
        y_ps = signal("y_ps", NT)
        ys = signal("ys", NT)
        yrelu = signal("yrelu", NT)
        h2s = signal("h2s", NT)
        h2T_ps = signal("h2T_ps", FT * NH)
        h2Ts = signal("h2Ts", FT * NH)
        x2_ps = signal("x2_ps", NT)
        x2s = signal("x2s", NT)
        a3_ps = signal("a3_ps", NT)
        v2s = signal("v2s", NT)
        a4_ps = signal("a4_ps", NT)
        x2f = signal("x2f", NT)
        qk3_ps = signal("qk3_ps", 2 * DT * NH)
        qk3s = signal("qk3s", 2 * DT * NH)
        v3_ps = signal("v3_ps", NT)
        v3s = signal("v3s", NT)
        s3_ps = signal("s3_ps", NH * NT)
        e3s = signal("e3s", NH * NT)
        p3s = signal("p3s", NH * NT)
        o3_ps = signal("o3_ps", NT)
        rd3 = signal("rd3", NT)
        x3s = signal("x3s", NT)

        NW = 5 + 6 + 5

        def stand(engine, waited):
            engine.sem_inc(waited.sem, 1)

        INVERT, WEIGH, SPREAD, NORMALISE, PROJECT, ADD = 5, 6, 8, 8, 9, 9
        PARTS = 2
        TBANKS = 3

        def group_due(u, lag):
            g, rest = divmod(u - lag, HPG)
            return g if rest == 0 and 0 <= g < NT * GROUPS else None

        def transposed_bank(n):
            return 4 + n % TBANKS

        def evacuates_both(u):
            return u % HEADS == HEADS - 1

        def by_act(u):
            return u + 1 + (u + 1) // HEADS

        def by_dve(u):
            return u + 1 - (u + 1) // HEADS

        def rows(t):
            return slice(t * P, (t + 1) * P)

        def half(n):
            return slice(n * HALF, (n + 1) * HALF)

        def heads_of(t):
            return t[:, :].rearrange("p (a n) -> p a n", n=P)

        block = ctx.enter_context(nc.Block())

        @block.sync
        def _(sp):
            def load(dst, src):
                sp.dma_start(dst, src).then_inc(weights_in.sem, 16)

            load(wqk0s[:], wqkT0.rearrange("(t p) d -> p t d", p=P))
            load(W0[:, :, D:2 * D], wv0.rearrange("(t p) d -> p t d", p=P))
            load(Wo1[:], w1attn[3].rearrange("(t p) d -> p t d", p=P))
            load(W1h[:], w1T.rearrange("(t p) d -> p t d", p=P))
            load(W2g[:], w2T.rearrange("(t p) d -> p t d", p=P))
            for dst, src in ((bq1c, bq1), (bk1c, bk1), (bq3c, bq3), (bk3c, bk3), (gammac, gamma), (betac, beta)):
                load(dst[:], src)
            for dst, src in ((bv1B, bv1), (bo1B, bo1), (b1B, b1), (b2B, b2), (bv3B, bv3)):
                load(dst[:], src.partition_broadcast(P))

            def load_x(b):
                sp.dma_start(xn[:], x_in[bass.ds(b, 1)].rearrange("o (t p) d -> p (o t) d", p=P)).then_inc(x_in_s.sem, 16)
                sp.dma_start(mask[:], mask_in[bass.ds(b, 1)].rearrange("o p t -> p (o t)")).then_inc(x_in_s.sem, 16)

            def load_adj(b):
                sp.dma_start(adjN[:], adj_in[bass.ds(b, 1)].rearrange("o (t p) n -> p (o t) n", p=P)).then_inc(adj_in_s.sem, 16)

            def load_w1():
                for i in range(3):
                    sp.dma_start(W1[:, i], w1attn[i].rearrange("(t p) d -> p t d", p=P)).then_inc(w1_in.sem, 16)

            load_w1()
            sp.sem_inc(x_free.sem, 1)
            sp.wait_ge(setup_dve.sem, 3)
            load_x(0)
            load_adj(0)

            def batch(b, last):
                sp.wait_ge(*lo_s(b, GROUPS * NH))
                stand(sp, waited_sp)
                sp.wait_ge(*vs(b, NT))
                stand(sp, waited_sp)
                for dst, parts, done in ((kS, (khi, khi, klo, klo), kS_in), (qS, (qhi, qlo, qhi, qlo), qS_in)):
                    if done is qS_in:
                        sp.wait_ge(*lo_s(b, 2 * GROUPS * NH))
                        stand(sp, waited_sp)
                    for r, src in enumerate(parts):
                        for j in range(HPG):
                            to = dst[HD * r:HD * r + HD].rearrange("p (g j) n -> p g j n", j=HPG)[:, :, j]
                            sp.dma_start(to.bitcast(F32), src[HD * j:HD * j + HD].bitcast(F32)).then_inc(done.sem, 16)
                sp.wait_ge(*pv_ps(b, NT * GROUPS))
                stand(sp, waited_sp)
                if not last:
                    load_w1()
                sp.dma_start(W1h[:], w1T.rearrange("(t p) d -> p t d", p=P)).then_inc(w2_in.sem, 16)
                sp.dma_start(W2g[:], w2T.rearrange("(t p) d -> p t d", p=P)).then_inc(w2_in.sem, 16)
                sp.dma_start(wB[:], adj_in[bass.ds(b, 1)][0, 0].partition_broadcast(P)).then_inc(wB_in.sem, 16)
                sp.wait_ge(*a4_ps(b, NT))
                stand(sp, waited_sp)
                for i, w in enumerate(w3attn):
                    sp.dma_start(W3[:, i], w.rearrange("(t p) d -> p t d", p=P)).then_inc(w3_in.sem, 16)
                if not last:
                    load_x(b + 1)
                    load_adj(b + 1)
                sp.wait_ge(*x3s(b, NT))
                stand(sp, waited_sp)
                sp.dma_start(out[bass.ds(b, 1)].rearrange("o (t p) d -> p (o t) d", p=P), x[:]).then_inc(out_s.sem, 16)
                sp.wait_ge(*out_s(b, 16))
                sp.sem_inc(x_free.sem, 1)

            with sp.Fori(0, B - 1) as b:
                batch(b, False)
            batch(B - 1, True)

        @block.gpsimd
        def _(pool):
            pool.memset(ident[:], 0.0).then_inc(consts_ready.sem, 1)
            pool.wait_ge(consts_ready.sem, 1)
            pool.affine_select(out=ident[:], in_=ident[:], compare_op=ALU.not_equal, fill=1.0, base=0,
                               pattern=[[-1, P]], channel_multiplier=1).then_inc(consts_ready.sem, 1)
            pool.memset(ones[:], 1.0).then_inc(consts_ready.sem, 1)
            pool.memset(mhalf[:], -0.5).then_inc(consts_ready.sem, 1)
            pool.wait_ge(consts_ready.sem, 4)

            def norm_scale(b, l):
                pool.wait_ge(*mvs(b, NT * (l + 1)))
                stand(pool, waited_pool)
                pool.tensor_scalar(ve[:], mv[:, :, 1], EPS, 1.0, ALU.add, ALU.mult).then_inc(ves.sem, 1)
                pool.wait_ge(*ves(b, l + 1))
                pool.tensor_tensor(rstd[:], ve[:], mhalf[:], ALU.pow).then_inc(rstds.sem, 1)

            with pool.Fori(0, B) as b:
                norm_scale(b, 0)
                norm_scale(b, 1)
                pool.wait_ge(*hs(b, 2 * NT))
                pool.tensor_tensor(x[:], x[:], bo1B[:].unsqueeze(1).broadcast_to([P, NT, D]), ALU.add).then_inc(xbo.sem, 1)
                norm_scale(b, 2)
                pool.wait_ge(*S_ps(b, UNITS))
                stand(pool, waited_pool)
                pool.memset(h[:, :, D:HW], 1.0).then_inc(ones_col.sem, 1)
                pool.wait_ge(*hs(b, 3 * NT))
                pool.tensor_tensor(x[:], x[:], h[:, :, 0:D], ALU.add).then_inc(xh.sem, 1)
                pool.wait_ge(*xh(b, 1))
                pool.tensor_tensor(x[:], x[:], b2B[:].unsqueeze(1).broadcast_to([P, NT, D]), ALU.add).then_inc(xhb.sem, 1)
                norm_scale(b, 3)
                pool.wait_ge(*a4_ps(b, NT))
                stand(pool, waited_pool)
                pool.memset(v3[:, :, D:HW], 1.0).then_inc(ones_col.sem, 1)
                norm_scale(b, 4)

        @block.vector
        def _(dve):
            dve.wait_ge(weights_in.sem, 16 * NW)
            for t in range(FT):
                dve.tensor_copy(betaB[:, t], betac[:, t:t + 1].broadcast_to([P, P])).then_inc(beta_bc.sem, 1)
            dve.wait_ge(setup_pe.sem, 1)
            dve.tensor_copy(W0[:, 0, 0:D], ps[:, 0, 0:D]).then_inc(setup_dve.sem, 1)
            dve.tensor_copy(W0[:, 1, 0:D], ps[:, 1, 0:D]).then_inc(setup_dve.sem, 1)
            dve.wait_ge(setup_pe.sem, 2)
            dve.tensor_copy(cB[:], ps[:, 2, 0:D]).then_inc(setup_dve.sem, 1)

            def statistics(b, l, t, src):
                dve.bn_stats(stats[:, t], src).then_inc(stat.sem, 1)

            def aggregate(b, l):
                for t in range(NT):
                    dve.wait_ge(*stat(b, NT * l + t + 1))
                    stand(dve, waited_dve)
                    dve.bn_aggr(mv[:, t], stats[:, t]).then_inc(mvs.sem, 1)
                dve.wait_ge(*rstds(b, l + 1))
                dve.wait_ge(*mvs(b, NT * (l + 1)))
                dve.scalar_tensor_tensor(nmr[:], mv[:, :, 0], -1.0, rstd[:], ALU.mult, ALU.mult).then_inc(nmrs.sem, 1)

            def hT_copies(b, n):
                for s in range(NH):
                    for c in range(DT):
                        k = n * 2 * DT + s * DT + c
                        dve.wait_ge(*hT_ps(b, k + 1))
                        dve.tensor_copy(hT[:, c, half(s)], ps[:, 4 + 2 * s + c]).then_inc(hTs.sem, 1)

            def batch(b):
                dve.wait_ge(*x_in_s(b, 32))
                for t in range(NT):
                    statistics(b, 0, t, xn[:, t])
                aggregate(b, 0)
                dve.tensor_scalar(mask16[:], mask[:], W_SCALE, None, ALU.mult).then_inc(chain.sem, 1)
                for n in range(1, NT * NH, 2):
                    dve.wait_ge(*aT_ps(b, n + 1))
                    jt, s = n // NH, n % NH
                    dve.tensor_copy(adjT[:, jt, half(s)], ps[:, n % 4]).then_inc(aT_dve.sem, 1)
                hT_copies(b, 0)
                for t in range(NT):
                    dve.wait_ge(*hs(b, t + 1))
                    dve.tensor_scalar(mh[:, t], h[:, t, 0:D], mask[:, t:t + 1], None, ALU.mult).then_inc(mhs.sem, 1)
                for t in range(NT):
                    dve.wait_ge(*agg_ps(b, t + 1))
                    dve.wait_ge(*gvs(b, t + 1))
                    if t:
                        dve.wait_ge(*wrs(b, t))
                    dve.tensor_tensor_reduce(E3[:, 0, 0:D], ps[:, 6 + t % 2, 0:D], GV[:, t, 0:D], 1.0, 0.0,
                                             ALU.mult, ALU.add, sw[:, 0, t:t + 1]).then_inc(wrs.sem, 1)
                dve.wait_ge(*wrs(b, NT))
                dve.wait_ge(*chain(b, 1))
                dve.tensor_tensor(sw[:, 1], sw[:, 0], mask16[:], ALU.mult).then_inc(chain.sem, 1)
                dve.wait_ge(*chain(b, 2))
                dve.reduce_max(s1[:, 0:1], sw[:, 1], AX.X).then_inc(chain.sem, 1)
                dve.wait_ge(*chain(b, 3))
                dve.tensor_copy(E3[:, 1, 0:P], s1[:, 0:1].broadcast_to([P, P])).then_inc(wm_bc.sem, 1)
                dve.wait_ge(*wmT_ps(b, 1))
                dve.tensor_reduce(s1[:, 1:2], ps[:, 4, 0:P], AX.X, ALU.max, negate=True).then_inc(nwms.sem, 1)
                dve.wait_ge(*esum_ps(b, 1))
                dve.reciprocal(s1[:, 3:4], ps[:, 5, 0:1]).then_inc(chain.sem, 1)
                dve.wait_ge(*chain(b, 4))
                dve.tensor_scalar(sw[:, 3], sw[:, 2], s1[:, 3:4], None, ALU.mult).then_inc(chain.sem, 1)
                dve.wait_ge(*chain(b, 5))
                dve.wait_ge(*x_free(b, 1))
                for t in range(NT):
                    dve.scalar_tensor_tensor(x[:, t], GV[:, t, D:2 * D], sw[:, 3, t:t + 1], xn[:, t],
                                             ALU.mult, ALU.add).then_inc(x0s.sem, 1)
                for t in range(NT):
                    dve.wait_ge(*x0s(b, t + 1))
                    statistics(b, 1, t, x[:, t])
                aggregate(b, 1)
                hT_copies(b, 1)
                for t in range(NT):
                    dve.wait_ge(*v_ps(b, t + 1))
                    dve.tensor_tensor(v[:, t], ps[:, t % 4, 0:D], bv1B[:], ALU.add).then_inc(vs.sem, 1)
                for n in range(2 * GROUPS * NH):
                    bias, hi, lo = ((bk1c, khi, klo), (bq1c, qhi, qlo))[n // (GROUPS * NH)]
                    g, s = n % (GROUPS * NH) // NH, n % NH
                    dve.wait_ge(*hi_s(b, n + 1))
                    dve.scalar_tensor_tensor(lo[:, g, half(s)], ps[:, 4 + n % 4], bias[:, g:g + 1],
                                             hi[:, g, half(s)].bitcast(F32), ALU.add, ALU.subtract).then_inc(lo_s.sem, 1)

                def evacuate(u):
                    if evacuates_both(u):
                        return
                    bank = transposed_bank(2 * u + 1)
                    dve.wait_ge(*T_ps(b, 2 * u + 2))
                    if u >= PTS:
                        dve.wait_ge(*pv_ps(b, (u - PTS) // HPG + 1))
                    dve.tensor_copy(PT[:, u % PTS, NT // 2:NT], heads_of(ps[:, bank])).then_inc(PT_dve.sem, 1)

                def inverse_sums(g):
                    dve.wait_ge(*exps(b, HPG * (g + 1)))
                    if g >= 2:
                        dve.wait_ge(*R_ps(b, g - 1))
                    dve.reciprocal(rs[:, g % 2], sm[:, HPG * g:HPG * g + HPG].unsqueeze(2).broadcast_to([P, HPG, HD])).then_inc(rss.sem, 1)

                def normalise(g):
                    dve.wait_ge(*pv_ps(b, g + 1))
                    dve.wait_ge(*Rss(b, g + 1))
                    if g >= GROUPS:
                        dve.wait_ge(*o_ps(b, (g - GROUPS) // GROUPS + 1))
                    dve.tensor_tensor(ctxn[:, g % GROUPS], ps[:, 7, 0:P], Rs[:], ALU.mult).then_inc(ctxs.sem, 1)

                def add_output(t):
                    dve.wait_ge(*o_ps(b, t + 1))
                    if t == 0:
                        dve.wait_ge(*xbo(b, 1))
                    dve.tensor_tensor(x[:, t], ps[:, 7, 2 * P:4 * P], x[:, t], ALU.add).then_inc(x1s.sem, 1)

                for u in range(UNITS + HEADS):
                    if u < UNITS:
                        dve.wait_ge(*S_ps(b, u + 1))
                        if u >= ZS:
                            dve.wait_ge(*T_ps(b, 2 * (u - ZS) + 2))
                        stand(dve, waited_dve)
                        dve.tensor_tensor_reduce(Z[:, u % ZS], ps[:, 2 * (u % 2):2 * (u % 2) + 2].rearrange("p a n -> p (a n)"),
                                                 adjN[:, u // HEADS], SCORE_SCALE, LOWEST, ALU.mult, ALU.max,
                                                 mx[:, u:u + 1]).then_inc(zs.sem, 1)
                    if 2 <= u < UNITS + 2:
                        evacuate(u - 2)
                    if u < UNITS:
                        dve.wait_ge(*zs(b, u + 1))
                        dve.tensor_scalar(nm[:, u:u + 1], mx[:, u:u + 1], -1.0, None, ALU.mult).then_inc(nms.sem, 1)
                    if (g := group_due(u, INVERT)) is not None:
                        inverse_sums(g)
                    if (g := group_due(u, NORMALISE)) is not None:
                        normalise(g)
                    if (g := group_due(u, ADD)) is not None and g % GROUPS == GROUPS - 1:
                        add_output(g // GROUPS)

                for t in range(NT):
                    dve.wait_ge(*x1s(b, t + 1))
                    statistics(b, 2, t, x[:, t])
                aggregate(b, 2)
                dve.wait_ge(*wB_in(b, 16))
                for t in range(NT):
                    if t:
                        dve.wait_ge(*dns(b, t))
                    dve.scalar_tensor_tensor(junk[:], adjN[:, t], 0.0, wB[:], ALU.not_equal, ALU.mult,
                                             accum_out=dn[:, 0, t:t + 1]).then_inc(dns.sem, 1)
                    dve.wait_ge(*dns(b, t + 1))
                    dve.tensor_scalar(H[:, t], adjN[:, t], 0.0, None, ALU.not_equal).then_inc(Hs.sem, 1)
                dve.tensor_scalar(dn[:, 1], dn[:, 0], 0.0, None, ALU.is_gt).then_inc(chain.sem, 1)
                dve.tensor_scalar(dn[:, 2], dn[:, 0], TINY, None, ALU.max).then_inc(chain.sem, 1)
                dve.wait_ge(*chain(b, 7))
                dve.reciprocal(dn[:, 3], dn[:, 2]).then_inc(chain.sem, 1)
                dve.wait_ge(*chain(b, 8))
                dve.tensor_tensor(dn[:, 3], dn[:, 3], dn[:, 1], ALU.mult).then_inc(chain.sem, 1)
                for t in range(NT):
                    dve.tensor_scalar(HT[:, t], adjT[:, t], 0.0, None, ALU.not_equal).then_inc(HTs.sem, 1)
                dve.wait_ge(*w2_in(b, 32))
                for t in range(FT):
                    dve.tensor_scalar(W2g[:, t], W2g[:, t], gammac[:, t:t + 1], None, ALU.mult).then_inc(w2g_s.sem, 1)
                for t in range(NT):
                    dve.wait_ge(*a1_ps(b, t + 1))
                    dve.tensor_scalar(be[:, 0, t:t + 1], ps[:, t % 2, D:D + 1], 1.0, None, ALU.max).then_inc(be_a.sem, 1)
                    dve.wait_ge(*be_a(b, t + 1))
                    dve.reciprocal(be[:, 1, t:t + 1], be[:, 0, t:t + 1]).then_inc(be_b.sem, 1)
                    dve.wait_ge(*be_b(b, t + 1))
                    dve.tensor_scalar(U[:, t], ps[:, t % 2, 0:D], be[:, 1, t:t + 1], None, ALU.mult).then_inc(Us.sem, 1)
                dve.wait_ge(*chain(b, 9))
                for t in range(NT):
                    dve.wait_ge(*y_ps(b, t + 1))
                    dve.scalar_tensor_tensor(h2[:, t], ps[:, t % 2], dn[:, 3, t:t + 1], b1B[:], ALU.mult,
                                             ALU.add).then_inc(ys.sem, 1)
                    if t:
                        dve.wait_ge(*yrelu(b, t))
                        statistics(b, 3, t - 1, h2[:, t - 1])
                dve.wait_ge(*yrelu(b, NT))
                statistics(b, 3, NT - 1, h2[:, NT - 1])
                aggregate(b, 3)
                for n in range(FT * NH):
                    dve.wait_ge(*h2T_ps(b, n + 1))
                    f, s = n % FT, n // FT
                    dve.tensor_copy(h2T[:, f, half(s)], ps[:, 2 + n % 4]).then_inc(h2Ts.sem, 1)
                for t in range(NT):
                    dve.wait_ge(*x2_ps(b, t + 1))
                    dve.tensor_tensor(U[:, t], ps[:, t % 2, 0:D], cB[:], ALU.add).then_inc(x2s.sem, 1)
                dve.wait_ge(*xhb(b, 1))
                for t in range(NT):
                    dve.wait_ge(*a4_ps(b, t + 1))
                    dve.scalar_tensor_tensor(x[:, t], ps[:, 4 + t % 2, 0:D], dn[:, 3, t:t + 1], x[:, t], ALU.mult,
                                             ALU.add).then_inc(x2f.sem, 1)
                for t in range(NT):
                    dve.wait_ge(*x2f(b, t + 1))
                    statistics(b, 4, t, x[:, t])
                aggregate(b, 4)
                hT_copies(b, 2)
                for t in range(NT):
                    dve.wait_ge(*v3_ps(b, t + 1))
                    if t == 0:
                        dve.wait_ge(*ones_col(b, 2))
                    dve.tensor_tensor(v3[:, t, 0:D], ps[:, t % 4, 0:D], bv3B[:], ALU.add).then_inc(v3s.sem, 1)

                def mask_exp(n):
                    s, kt = n // NT, n % NT
                    dve.wait_ge(*e3s(b, n + 1))
                    dve.tensor_tensor(P3[:, s, kt], E3[:, n % 2], adjT[:, kt, half(s)], ALU.mult).then_inc(p3s.sem, 1)

                def finish(t):
                    dve.wait_ge(*o3_ps(b, t + 1))
                    dve.reciprocal(rden[:, t:t + 1], ps[:, 4 + t % 2, D:D + 1]).then_inc(rd3.sem, 1)
                    dve.wait_ge(*rd3(b, t + 1))
                    dve.scalar_tensor_tensor(x[:, t], ps[:, 4 + t % 2, 0:D], rden[:, t:t + 1], x[:, t], ALU.mult,
                                             ALU.add).then_inc(x3s.sem, 1)

                for n in range(NH * NT):
                    mask_exp(n)
                for t in range(NT):
                    finish(t)

            with dve.Fori(0, B) as b:
                batch(b)

        @block.scalar
        def _(act):
            def normalise(b, l, k, src):
                act.wait_ge(*nmrs(b, l + 1))
                for t in range(NT):
                    act.activation(h[:, t, 0:D], src[:, t], ACT.Relu, bias=nmr[:, t:t + 1],
                                   scale=rstd[:, t:t + 1]).then_inc(hs.sem, 1)

            def batch(b):
                for n in range(0, NT * NH, 2):
                    act.wait_ge(*aT_ps(b, n + 1))
                    jt, s = n // NH, n % NH
                    act.activation(adjT[:, jt, half(s)], ps[:, n % 4], ACT.Copy).then_inc(aT_act.sem, 1)
                normalise(b, 0, 0, xn)
                for t in range(NT):
                    act.wait_ge(*gv_ps(b, t + 1))
                    act.activation(GV[:, t], ps[:, 4 + t % 2], ACT.Copy).then_inc(gvs.sem, 1)
                act.wait_ge(*nwms(b, 1))
                act.activation(sw[:, 2], sw[:, 1], ACT.Exp, bias=s1[:, 1:2], accum_out=s1[:, 2:3]).then_inc(es.sem, 1)
                normalise(b, 1, 1, x)
                for n in range(2 * GROUPS * NH):
                    bias, hi = ((bk1c, khi), (bq1c, qhi))[n // (GROUPS * NH)]
                    g, s = n % (GROUPS * NH) // NH, n % NH
                    act.wait_ge(*kq_ps(b, n + 1))
                    act.activation(hi[:, g, half(s)], ps[:, 4 + n % 4], ACT.Identity, bias=bias[:, g:g + 1]).then_inc(hi_s.sem, 1)

                def evacuate(u):
                    for half_of_u in range(1 + evacuates_both(u)):
                        bank = transposed_bank(2 * u + half_of_u)
                        act.wait_ge(*T_ps(b, 2 * u + half_of_u + 1))
                        if u >= PTS:
                            act.wait_ge(*pv_ps(b, (u - PTS) // HPG + 1))
                        first = NT // 2 * half_of_u
                        act.activation(PT[:, u % PTS, first:first + NT // 2], heads_of(ps[:, bank]), ACT.Copy).then_inc(PT_act.sem, 1)

                for u in range(UNITS + HEADS):
                    if u < UNITS:
                        act.wait_ge(*nms(b, u + 1))
                        act.activation(Z[:, u % ZS], Z[:, u % ZS], ACT.Exp, bias=nm[:, u:u + 1],
                                       accum_out=sm[:, u:u + 1]).then_inc(exps.sem, 1)
                    if 1 <= u < UNITS + 1:
                        evacuate(u - 1)
                    if (g := group_due(u, SPREAD)) is not None:
                        act.wait_ge(*R_ps(b, g + 1))
                        if g:
                            act.wait_ge(*ctxs(b, g))
                        act.activation(Rs[:], ps[:, 7, P:2 * P], ACT.Copy).then_inc(Rss.sem, 1)
                normalise(b, 2, 2, x)
                for n in range(DT * NH):
                    act.wait_ge(*a2_ps(b, n + 1))
                    act.activation(A2T[:, n // NH, half(n % NH)], ps[:, 2 + n % 4], ACT.Copy).then_inc(a2s.sem, 1)
                for t in range(NT):
                    act.wait_ge(*ys(b, t + 1))
                    act.activation(h2[:, t], h2[:, t], ACT.Relu).then_inc(yrelu.sem, 1)
                act.wait_ge(*nmrs(b, 4))
                for t in range(NT):
                    act.activation(h2[:, t], h2[:, t], ACT.Identity, bias=nmr[:, t:t + 1],
                                   scale=rstd[:, t:t + 1]).then_inc(h2s.sem, 1)
                for t in range(NT):
                    act.wait_ge(*a3_ps(b, t + 1))
                    act.activation(A2T[:].rearrange("p c n -> p (c n)")[:, D * t:D * t + D], ps[:, 2 + t % 2, 0:D], ACT.Copy,
                                   scale=be[:, 1, t:t + 1]).then_inc(v2s.sem, 1)
                normalise(b, 4, 3, x)
                for n in range(2 * DT * NH):
                    bias, dst = ((bk3c, k3T), (bq3c, q3T))[n // (DT * NH)]
                    f, s = n % (DT * NH) // NH, n % NH
                    act.wait_ge(*qk3_ps(b, n + 1))
                    act.activation(dst[:, f, half(s)], ps[:, 4 + n % 4], ACT.Identity, bias=bias[:, f:f + 1]).then_inc(qk3s.sem, 1)
                for n in range(NH * NT):
                    act.wait_ge(*s3_ps(b, n + 1))
                    if n >= 2:
                        act.wait_ge(*p3s(b, n - 1))
                    act.activation(E3[:, n % 2], ps[:, n % 4], ACT.Exp).then_inc(e3s.sem, 1)

            with act.Fori(0, B) as b:
                batch(b)

        @block.tensor
        def _(pe):
            def product(dst, pairs):
                for i, (lhsT, rhs) in enumerate(pairs):
                    mm = pe.matmul(dst, lhsT, rhs, start=(i == 0), stop=(i == len(pairs) - 1))
                return mm

            pe.wait_ge(weights_in.sem, 16 * NW)
            for a in range(DT):
                mm = product(ps[:, a, 0:D], [(wqk0s[:, c, rows(a)], wqk0s[:, DT + c]) for c in range(DT)])
            mm.then_inc(setup_pe.sem, 1)
            pe.wait_ge(consts_ready.sem, 4)
            pe.wait_ge(beta_bc.sem, FT)
            product(ps[:, 2, 0:D], [(betaB[:, t], W2g[:, t]) for t in range(FT)]).then_inc(setup_pe.sem, 1)
            pe.wait_ge(setup_dve.sem, 3)

            def transpose_h(b, k, n):
                for s in range(NH):
                    for c in range(DT):
                        for a in range(TPH):
                            t = TPH * s + a
                            pe.wait_ge(*hs(b, NT * k + t + 1))
                            mm = pe.transpose(ps[:, 4 + 2 * s + c, rows(a)], h[:, t, rows(c)], ident[:])
                        mm.then_inc(hT_ps.sem, 1)

            def batch(b):
                pe.wait_ge(*adj_in_s(b, 16))
                for n in range(NT * NH):
                    jt, s = n // NH, n % NH
                    if n >= 4:
                        done = aT_act if n % 2 == 0 else aT_dve
                        pe.wait_ge(*done(b, (n - 4) // 2 + 1))
                    for a in range(TPH):
                        mm = pe.transpose(ps[:, n % 4, rows(a)], adjN[:, TPH * s + a, rows(jt)], ident[:])
                    mm.then_inc(aT_ps.sem, 1)
                transpose_h(b, 0, 0)
                pe.wait_ge(*hTs(b, 2 * DT))
                for t in range(NT):
                    if t >= 2:
                        pe.wait_ge(*gvs(b, t - 1))
                    product(ps[:, 4 + t % 2], [(hT[:, c, rows(t)], W0[:, c]) for c in range(DT)]).then_inc(gv_ps.sem, 1)
                pe.wait_ge(*mhs(b, NT))
                pe.wait_ge(*aT_act(b, NT * NH // 2))
                pe.wait_ge(*aT_dve(b, NT * NH // 2))
                for t in range(NT):
                    if t >= 2:
                        pe.wait_ge(*wrs(b, t - 1))
                    product(ps[:, 6 + t % 2, 0:D], [(adjT[:, j, rows(t)], mh[:, j]) for j in range(NT)]).then_inc(agg_ps.sem, 1)
                pe.wait_ge(*wm_bc(b, 1))
                pe.wait_ge(*gvs(b, NT))
                pe.transpose(ps[:, 4, 0:P], E3[:, 1, 0:P], ident[:]).then_inc(wmT_ps.sem, 1)
                pe.wait_ge(*es(b, 1))
                pe.matmul(ps[:, 5, 0:1], ones[:], s1[:, 2:3], start=True, stop=True).then_inc(esum_ps.sem, 1)
                transpose_h(b, 1, 1)
                pe.wait_ge(*hTs(b, 4 * DT))
                pe.wait_ge(*w1_in(b, 48))
                for t in range(NT):
                    if t >= 4:
                        pe.wait_ge(*vs(b, t - 3))
                    product(ps[:, t % 4, 0:D], [(hT[:, c, rows(t)], Wv1[:, c]) for c in range(DT)]).then_inc(v_ps.sem, 1)
                for n in range(2 * GROUPS * NH):
                    w = (Wk1, Wq1)[n // (GROUPS * NH)]
                    g, s = n % (GROUPS * NH) // NH, n % NH
                    if n >= 4:
                        pe.wait_ge(*lo_s(b, n - 3))
                    product(ps[:, 4 + n % 4], [(w[:, c, rows(g)], hT[:, c, half(s)]) for c in range(DT)]).then_inc(kq_ps.sem, 1)

                def scores(u):
                    t, hd = u // HEADS, u % HEADS
                    if u >= 2:
                        pe.wait_ge(*zs(b, u - 1))
                    for s in range(NH):
                        mm = pe.matmul(ps[:, 2 * (u % 2) + s], qS[:, hd, rows(t)], kS[:, hd, half(s)], start=True, stop=True)
                    mm.then_inc(S_ps.sem, 1)

                def transposes(u):
                    pe.wait_ge(*exps(b, u + 1))
                    for s in range(2):
                        n = 2 * u + s
                        if n >= TBANKS:
                            before, s_before = divmod(n - TBANKS, 2)
                            if s_before == 0 or evacuates_both(before):
                                pe.wait_ge(*PT_act(b, by_act(before) - (s_before == 0 and evacuates_both(before))))
                            else:
                                pe.wait_ge(*PT_dve(b, by_dve(before)))
                        for a in range(NT // 2):
                            mm = pe.transpose(ps[:, transposed_bank(n), rows(a)], Z[:, u % ZS, rows(NT // 2 * s + a)], ident[:])
                        mm.then_inc(T_ps.sem, 1)

                def weighted_values(g, part):
                    if part == 0:
                        pe.wait_ge(*PT_act(b, by_act(HPG * g + HPG - 1)))
                        pe.wait_ge(*PT_dve(b, by_dve(HPG * g + HPG - 1)))
                        if g >= 1 and g % GROUPS:
                            pe.wait_ge(*ctxs(b, g))
                        elif g >= 1:
                            pe.wait_ge(*x1s(b, g // GROUPS))
                    for kt in range(NT // PARTS * part, NT // PARTS * (part + 1)):
                        for j in range(HPG):
                            hd = HPG * (g % GROUPS) + j
                            mm = pe.matmul(ps[HD * j:HD * j + HD, 7, 0:P],
                                           v[:, kt, HD * hd:HD * hd + HD], PT[:, (HPG * g + j) % PTS, kt],
                                           start=(kt == 0), stop=(kt == NT - 1))
                    if part < PARTS - 1:
                        return
                    mm.then_inc(pv_ps.sem, 1)
                    pe.wait_ge(*rss(b, g + 1))
                    pe.matmul(ps[:, 7, P:2 * P], rs[:, g % 2].rearrange("p h d -> p (h d)"),
                              ident[:], start=True, stop=True).then_inc(R_ps.sem, 1)

                def project(t):
                    pe.wait_ge(*ctxs(b, GROUPS * (t + 1)))
                    product(ps[:, 7, 2 * P:4 * P], [(ctxn[:, g], Wo1[:, g]) for g in range(GROUPS)]).then_inc(o_ps.sem, 1)

                pe.wait_ge(*kS_in(b, 256))
                pe.wait_ge(*qS_in(b, 256))
                pe.wait_ge(*lo_s(b, 2 * GROUPS * NH))
                scores(0)
                scores(1)
                for u in range(UNITS + HEADS):
                    if u + 2 < UNITS:
                        scores(u + 2)
                    if (g := group_due(u, PROJECT)) is not None and g % GROUPS == GROUPS - 1:
                        project(g // GROUPS)
                    for part in range(PARTS):
                        if (g := group_due(u, WEIGH + part)) is not None:
                            weighted_values(g, part)
                    if u < UNITS:
                        transposes(u)
                pe.wait_ge(*hs(b, 3 * NT))
                pe.wait_ge(*ones_col(b, 1))
                pe.wait_ge(*Hs(b, NT))
                for t in range(NT):
                    if t >= 2:
                        pe.wait_ge(*Us(b, t - 1))
                    product(ps[:, t % 2, 0:HW], [(H[:, j, rows(t)], h[:, j]) for j in range(NT)]).then_inc(a1_ps.sem, 1)
                pe.wait_ge(*HTs(b, NT))
                pe.wait_ge(*Us(b, NT))
                for n in range(DT * NH):
                    product(ps[:, 2 + n % 4], [(U[:, j, rows(n // NH)], HT[:, j, half(n % NH)]) for j in range(NT)]).then_inc(a2_ps.sem, 1)
                pe.wait_ge(*a2s(b, DT * NH))
                for t in range(NT):
                    if t >= 2:
                        pe.wait_ge(*ys(b, t - 1))
                    product(ps[:, t % 2], [(A2T[:, c, rows(t)], W1h[:, c]) for c in range(DT)]).then_inc(y_ps.sem, 1)
                for n in range(FT * NH):
                    f, s = n % FT, n // FT
                    if n >= 4:
                        pe.wait_ge(*h2Ts(b, n - 3))
                    for a in range(TPH):
                        if f == 0:
                            pe.wait_ge(*h2s(b, TPH * s + a + 1))
                        mm = pe.transpose(ps[:, 2 + n % 4, rows(a)], h2[:, TPH * s + a, rows(f)], ident[:])
                    mm.then_inc(h2T_ps.sem, 1)
                pe.wait_ge(*h2Ts(b, FT * NH))
                pe.wait_ge(*w2g_s(b, FT))
                for t in range(NT):
                    if t >= 2:
                        pe.wait_ge(*x2s(b, t - 1))
                    product(ps[:, t % 2, 0:D], [(h2T[:, f, rows(t)], W2g[:, f]) for f in range(FT)]).then_inc(x2_ps.sem, 1)
                pe.wait_ge(*x2s(b, NT))
                for t in range(NT):
                    if t >= 2:
                        pe.wait_ge(*v2s(b, t - 1))
                    product(ps[:, 2 + t % 2, 0:D], [(H[:, j, rows(t)], U[:, j]) for j in range(NT)]).then_inc(a3_ps.sem, 1)
                pe.wait_ge(*v2s(b, NT))
                V2 = A2T[:].rearrange("p c n -> p (c n)")
                for t in range(NT):
                    if t >= 2:
                        pe.wait_ge(*x2f(b, t - 1))
                    product(ps[:, 4 + t % 2, 0:D], [(HT[:, j, rows(t)], V2[:, D * j:D * j + D]) for j in range(NT)]).then_inc(a4_ps.sem, 1)
                transpose_h(b, 3, 2)
                pe.wait_ge(*hTs(b, 6 * DT))
                pe.wait_ge(*w3_in(b, 48))
                for t in range(NT):
                    if t >= 4:
                        pe.wait_ge(*v3s(b, t - 3))
                    product(ps[:, t % 4, 0:D], [(hT[:, c, rows(t)], W3[:, 2, c]) for c in range(DT)]).then_inc(v3_ps.sem, 1)
                for n in range(2 * DT * NH):
                    w = (1, 0)[n // (DT * NH)]
                    f, s = n % (DT * NH) // NH, n % NH
                    if n >= 4:
                        pe.wait_ge(*qk3s(b, n - 3))
                    product(ps[:, 4 + n % 4], [(W3[:, w, c, rows(f)], hT[:, c, half(s)]) for c in range(DT)]).then_inc(qk3_ps.sem, 1)
                pe.wait_ge(*qk3s(b, 2 * DT * NH))
                pe.wait_ge(*v3s(b, NT))
                for n in range(NH * NT):
                    s, kt = n // NT, n % NT
                    if n >= 4:
                        pe.wait_ge(*e3s(b, n - 3))
                    product(ps[:, n % 4], [(k3T[:, c, rows(kt)], q3T[:, c, half(s)]) for c in range(DT)]).then_inc(s3_ps.sem, 1)
                for t in range(NT):
                    s, a = t // TPH, t % TPH
                    pe.wait_ge(*p3s(b, NT * (s + 1)))
                    if t >= 2:
                        pe.wait_ge(*x3s(b, t - 1))
                    product(ps[:, 4 + t % 2, 0:D + 1], [(P3[:, s, j, rows(a)], v3[:, j, 0:D + 1]) for j in range(NT)]).then_inc(o3_ps.sem, 1)

            with pe.Fori(0, B) as b:
                batch(b)


def kernel(x, adj, nodemask, L0_gnn_Wqk, L0_gnn_Wv, L1_gnn_Wq, L1_gnn_bq, L1_gnn_Wk, L1_gnn_bk, L1_gnn_Wv,
           L1_gnn_bv, L1_gnn_Wo, L1_gnn_bo, L2_gnn_W1, L2_gnn_b1, L2_gnn_gamma, L2_gnn_beta, L2_gnn_W2, L2_gnn_b2,
           L3_gnn_Wq_w, L3_gnn_Wq_b, L3_gnn_Wk_w, L3_gnn_Wk_b, L3_gnn_Wv_w, L3_gnn_Wv_b):
    import numpy as np
    import concourse.bacc as bacc
    from concourse.bass_utils import run_bass_kernel_spmd

    def T(a):
        return np.ascontiguousarray(np.asarray(a).T)

    def columns(a):
        a = np.asarray(a)
        return np.swapaxes(a.reshape(*a.shape[:-1], -1, P), -1, -2)

    arrays = {
        "x_in": x, "adj_in": adj, "mask_in": columns(nodemask), "wqkT0": T(L0_gnn_Wqk), "wv0": L0_gnn_Wv,
        "wq1": T(L1_gnn_Wq), "wk1": T(L1_gnn_Wk), "wv1": T(L1_gnn_Wv), "wo1": T(L1_gnn_Wo),
        "bq1": columns(L1_gnn_bq), "bk1": columns(L1_gnn_bk), "bv1": L1_gnn_bv, "bo1": L1_gnn_bo,
        "w1T": T(L2_gnn_W1), "b1": L2_gnn_b1, "gamma": columns(L2_gnn_gamma), "beta": columns(L2_gnn_beta),
        "w2T": T(L2_gnn_W2), "b2": L2_gnn_b2,
        "wq3": T(L3_gnn_Wq_w), "wk3": T(L3_gnn_Wk_w), "wv3": T(L3_gnn_Wv_w),
        "bq3": columns(L3_gnn_Wq_b), "bk3": columns(L3_gnn_Wk_b), "bv3": L3_gnn_Wv_b,
    }
    arrays = {n: np.ascontiguousarray(a) for n, a in arrays.items()}
    nc = bacc.Bacc("TRN2", target_bir_lowering=False, num_devices=1)
    t = {n: nc.dram_tensor(n, a.shape, mybir.dt.from_np(a.dtype), kind="ExternalInput").ap() for n, a in arrays.items()}
    out = nc.dram_tensor("out", arrays["x_in"].shape, F32, kind="ExternalOutput").ap()
    build_program(nc, t["x_in"], t["adj_in"], t["mask_in"], t["wqkT0"], t["wv0"],
                  [t["wq1"], t["wk1"], t["wv1"], t["wo1"]], t["bq1"], t["bk1"], t["bv1"], t["bo1"],
                  t["w1T"], t["b1"], t["gamma"], t["beta"], t["w2T"], t["b2"],
                  [t["wq3"], t["wk3"], t["wv3"]], t["bq3"], t["bk3"], t["bv3"], out)
    r = run_bass_kernel_spmd(nc, [arrays], core_ids=[0])
    return r.results[0]["out"]
```

```python
from contextlib import ExitStack

import concourse.bass as bass
from concourse import mybir

F32 = mybir.dt.float32
F32R = mybir.dt.float32r
ALU = mybir.AluOpType
ACT = mybir.ActivationFunctionType
AX = mybir.AxisListType

P = 128
HALF = 512
EPS = 1e-5
LOWEST = -3.0e38
TINY = 1.2e-38


class Signal:

    def __init__(self, sem, per):
        self.sem, self.per = sem, per

    def __call__(self, b, n):
        return self.sem, b * self.per + n


def build_program(nc, x_in, adj_in, mask_in, wqkT0, wv0, w1attn, bq1, bk1, bv1, bo1,
                  w1T, b1, gamma, beta, w2T, b2, w3attn, bq3, bk3, bv3, out):
    B, N, D = x_in.shape
    NT = N // P
    DT = D // P
    NH = N // HALF
    TPH = HALF // P
    HID = w1T.shape[1]
    FT = HID // P
    HEADS = 8
    HD = D // HEADS
    HPG = P // HD
    GROUPS = HEADS // HPG
    UNITS = NT * HEADS
    PTS = 8
    ZS = 3
    SCORE_SCALE = 2.0 * float(HD) ** -0.5
    W_SCALE = 1.0 / float(D) ** 0.5

    ctx = ExitStack()
    with ctx:
        def sb(name, shape, dt=F32, scope=ctx):
            return scope.enter_context(nc.sbuf_tensor(name, shape, dt))

        def signal(name, per):
            return Signal(ctx.enter_context(nc.semaphore(name)), per)

        adjT = sb("adjT", [P, NT, N])
        x = sb("x", [P, NT, D])
        ident = sb("ident", [P, P])
        ones = sb("ones", [P, P])
        W0 = sb("W0", [P, DT, 2 * D])
        Wo1 = sb("Wo1", [P, DT, D])
        bq1c = sb("bq1c", [P, DT])
        bk1c = sb("bk1c", [P, DT])
        bq3c = sb("bq3c", [P, DT])
        bk3c = sb("bk3c", [P, DT])
        gammac = sb("gammac", [P, FT])
        betac = sb("betac", [P, FT])
        bv1B = sb("bv1B", [P, D])
        bo1B = sb("bo1B", [P, D])
        b1B = sb("b1B", [P, HID])
        b2B = sb("b2B", [P, D])
        bv3B = sb("bv3B", [P, D])
        cB = sb("cB", [P, D])
        mhalf = sb("mhalf", [P, NT])
        mask = sb("mask", [P, NT])
        mask16 = sb("mask16", [P, NT])
        stats = sb("stats", [P, NT, 6])
        mv = sb("mv", [P, NT, 2])
        ve = sb("ve", [P, NT])
        rstd = sb("rstd", [P, NT])
        nmr = sb("nmr", [P, NT])
        sw = sb("sw", [P, 4, NT])
        s1 = sb("s1", [P, 8])
        mx = sb("mx", [P, UNITS])
        nm = sb("nm", [P, UNITS])
        sm = sb("sm", [P, UNITS])
        rs = sb("rs", [P, HPG, HD])
        Rs = sb("Rs", [P, P])
        ctxn = sb("ctxn", [P, GROUPS, P])
        dn = sb("dn", [P, 4, NT])
        be = sb("be", [P, 2, NT])
        rden = sb("rden", [P, NT])

        def region(*layouts):
            got = []
            for i, layout in enumerate(layouts):
                with ExitStack() as scope:
                    got.append([sb(n if i == 0 else f"{n}_{i}", s, d, scope) for n, s, d in layout])
            sizes = [sum(_bytes(s) for _, s, _ in layout) for layout in layouts]
            sb(f"region_{layouts[0][0][0]}", [P, max(sizes) // 4])
            return got

        def _bytes(shape):
            n = 4
            for s in shape[1:]:
                n *= s
            return n

        (adj0, adj2) = region([("adjN", [P, NT, N], F32)],
                              [("H", [P, NT, N], F32R)])
        (adjN,), (H,) = adj0, adj2
        HW = D + 2
        common = [("h", [P, NT, HW], F32), ("hT", [P, DT, N], F32)]
        (a0, a1, a2, a3, asetup) = region(
            common + [("mh", [P, NT, D], F32), ("G", [P, NT, D], F32)],
            [("qS", [P, HEADS, N], F32R), ("kS", [P, HEADS, N], F32R)],
            common[:1] + [("HT", [P, NT, N], F32R), ("Uh", [P, NT, D], F32R), ("Ul", [P, NT, D], F32R),
                          ("A2T", [P, DT, N], F32)],
            common + [("q3T", [P, DT, N], F32), ("k3T", [P, DT, N], F32), ("v3", [P, NT, HW], F32),
                      ("W3", [P, 3, DT, D], F32)],
            [("wqk0s", [P, 4, D], F32), ("betaB", [P, FT, P], F32)],
        )
        h, hT, mh, G = a0
        qS, kS = a1
        _, HT, Uh, Ul, A2T = a2
        _, _, q3T, k3T, v3, W3 = a3
        wqk0s, betaB = asetup
        (p1a, p1b, p2, p2a, p2v, p3) = region(
            [("khi", [P, GROUPS, N], F32R), ("klo", [P, GROUPS, N], F32R),
             ("qhi", [P, GROUPS, N], F32R), ("qlo", [P, GROUPS, N], F32R), ("hT1", [P, DT, N], F32),
             ("W1", [P, 3, DT, D], F32)],
            [("PT", [P, PTS, NT, P], F32), ("Z", [P, ZS, N], F32)],
            [("h2", [P, NT, HID], F32), ("h2T", [P, FT, N], F32)],
            [("hh", [P, NT, HW], F32R), ("hl", [P, NT, D], F32R), ("wB", [P, N], F32), ("junk", [P, N], F32)],
            [("Vh", [P, NT, D], F32R), ("Vl", [P, NT, D], F32R)],
            [("P3", [P, NH, NT, HALF], F32), ("E3", [P, 2, HALF], F32)],
        )
        khi, klo, qhi, qlo, hT1, W1 = p1a
        PT, Z = p1b
        h2, h2T = p2
        hh, hl, wB, junk = p2a
        Vh, Vl = p2v
        P3, E3 = p3
        (r1, r2, r3) = region(
            [("v", [P, NT, D], F32)],
            [("W1h", [P, DT, HID], F32), ("W2g", [P, FT, D], F32)],
            [("xn", [P, NT, D], F32)],
        )
        (v,), (W1h, W2g), (xn,) = r1, r2, r3
        Wq1, Wk1, Wv1 = (W1[:, i] for i in range(3))

        ps = ctx.enter_context(nc.psum_tensor("ps", [P, 8, HALF], F32))

        weights_in = signal("weights_in", 0)
        consts_ready = signal("consts_ready", 0)
        beta_bc = signal("beta_bc", 0)
        setup_pe = signal("setup_pe", 0)
        setup_dve = signal("setup_dve", 0)
        waited_dve = signal("waited_dve", 0)
        waited_pool = signal("waited_pool", 0)
        waited_sp = signal("waited_sp", 0)
        adj_in_s = signal("adj_in_s", 16)
        x_in_s = signal("x_in_s", 32)
        out_s = signal("out_s", 16)
        x_free = signal("x_free", 1)
        kS_in = signal("kS_in", 256)
        qS_in = [signal(f"qS_in{j}", 64) for j in range(HPG)]
        w2_in = signal("w2_in", 32)
        wB_in = signal("wB_in", 16)
        w3_in = signal("w3_in", 48)
        w1_in = signal("w1_in", 48)
        stat = signal("stat", 5 * NT)
        mvs = signal("mvs", 5 * NT)
        ves = signal("ves", 5 * NH)
        rstds = signal("rstds", 5 * NH)
        nmrs = signal("nmrs", 5 * NH)
        hs = signal("hs", 3 * NT)
        hT_ps = signal("hT_ps", 3 * 2 * DT)
        hTs = signal("hTs", 3 * 2 * DT)
        aT_ps = signal("aT_ps", NT * NH)
        aT_act = signal("aT_act", NT * NH // 2)
        aT_dve = signal("aT_dve", NT * NH // 2)
        g_ps = signal("g_ps", NT)
        gs = signal("gs", NT)
        mhs = signal("mhs", NT)
        agg_ps = signal("agg_ps", NT)
        wrs = signal("wrs", NT)
        chain = signal("chain", 9)
        wm_bc = signal("wm_bc", 1)
        wmT_ps = signal("wmT_ps", 1)
        nwms = signal("nwms", 1)
        es = signal("es", 1)
        esum_ps = signal("esum_ps", 1)
        V_ps = signal("V_ps", NT)
        x0s = signal("x0s", NT)
        xbo = signal("xbo", 1)
        v_ps = signal("v_ps", NT)
        vs = signal("vs", NT)
        kq_ps = signal("kq_ps", 2 * GROUPS * NH)
        hi_s = signal("hi_s", 2 * GROUPS * NH)
        lo_s = signal("lo_s", 2 * GROUPS * NH)
        S_ps = signal("S_ps", UNITS)
        zs = signal("zs", UNITS)
        nms = signal("nms", UNITS)
        exps = signal("exps", UNITS)
        T_ps = signal("T_ps", 2 * UNITS)
        PT_act = signal("PT_act", UNITS + UNITS // 4)
        PT_dve = signal("PT_dve", UNITS - UNITS // 4)
        pv_ps = signal("pv_ps", NT * GROUPS)
        R_ps = signal("R_ps", NT * GROUPS)
        invs = signal("invs", NT * GROUPS)
        rss = signal("rss", NT * GROUPS)
        Rss = signal("Rss", NT * GROUPS)
        ctxs = signal("ctxs", NT * GROUPS)
        o_ps = signal("o_ps", NT)
        x1s = signal("x1s", NT)
        ones_col = signal("ones_col", 1)
        ones_h = signal("ones_h", 1)
        h_d = signal("h_d", NT)
        hhs = signal("hhs", NT)
        hls = signal("hls", NT)
        uhs = signal("uhs", NT)
        x2t = signal("x2t", NT)
        x2h = signal("x2h", NT)
        vhs = signal("vhs", NT)
        dns = signal("dns", NT)
        Hs = signal("Hs", NT)
        HTs = signal("HTs", NT)
        w2g_s = signal("w2g_s", FT)
        xh = signal("xh", 2)
        xhb = signal("xhb", 1)
        a1_ps = signal("a1_ps", NT)
        be_a = signal("be_a", NT)
        be_b = signal("be_b", NT)
        Us = signal("Us", NT)
        a2_ps = signal("a2_ps", DT * NH)
        a2s = signal("a2s", DT * NH)
        y_ps = signal("y_ps", NT)
        ys = signal("ys", NT)
        yrelu = signal("yrelu", NT)
        h2s = signal("h2s", NT)
        h2T_ps = signal("h2T_ps", FT * NH)
        h2Ts = signal("h2Ts", FT * NH)
        x2_ps = signal("x2_ps", NT)
        x2s = signal("x2s", NT)
        a3_ps = signal("a3_ps", NT)
        v2s = signal("v2s", NT)
        a4_ps = signal("a4_ps", NT)
        x2f = signal("x2f", NT)
        qk3_ps = signal("qk3_ps", 2 * DT * NH)
        qk3s = signal("qk3s", 2 * DT * NH)
        v3_ps = signal("v3_ps", NT)
        v3s = signal("v3s", NT)
        s3_ps = signal("s3_ps", NH * NT)
        e3s = signal("e3s", NH * NT)
        p3s = signal("p3s", NH * NT)
        o3_ps = signal("o3_ps", NT)
        rd3 = signal("rd3", NT)
        x3s = signal("x3s", NT)

        NW = 5 + 6 + 5

        def stand(engine, waited):
            engine.sem_inc(waited.sem, 1)

        INVERT, SPREAD, COPY, WEIGH, NORMALISE, PROJECT, ADD = 4, 5, 6, 6, 9, 10, 11
        PARTS = (3, 3, 2)
        STEPS = UNITS + HEADS + 2

        def group_due(u, lag):
            g, rest = divmod(u - lag, HPG)
            return g if rest == 0 and 0 <= g < NT * GROUPS else None

        def tile_due(u, lag):
            g = group_due(u, lag)
            return g // GROUPS if g is not None and g % GROUPS == GROUPS - 1 else None

        TBANKS = 3
        BOTH = 4
        turns = []
        for u in range(STEPS):
            if tile_due(u, PROJECT) is not None:
                turns.append((tile_due(u, PROJECT), "out"))
            if u < UNITS:
                turns += [(u, 0), (u, 1)]

        def turn_bank(use):
            return 4 + turns.index(use) % TBANKS

        def evacuates_both(u):
            return u % BOTH == BOTH - 1

        def by_act(u):
            return u + 1 + (u + 1) // BOTH

        def by_dve(u):
            return u + 1 - (u + 1) // BOTH

        def bank(t):
            return (4 + t) % NT

        def after(l, s):
            return NH * l + s + 1

        def rows(t):
            return slice(t * P, (t + 1) * P)

        def half(n):
            return slice(n * HALF, (n + 1) * HALF)

        def heads_of(t):
            return t[:, :].rearrange("p (a n) -> p a n", n=P)

        block = ctx.enter_context(nc.Block())

        @block.sync
        def _(sp):
            def load(dst, src):
                sp.dma_start(dst, src).then_inc(weights_in.sem, 16)

            load(wqk0s[:], wqkT0.rearrange("(t p) d -> p t d", p=P))
            load(W0[:, :, D:2 * D], wv0.rearrange("(t p) d -> p t d", p=P))
            load(Wo1[:], w1attn[3].rearrange("(t p) d -> p t d", p=P))
            load(W1h[:], w1T.rearrange("(t p) d -> p t d", p=P))
            load(W2g[:], w2T.rearrange("(t p) d -> p t d", p=P))
            for dst, src in ((bq1c, bq1), (bk1c, bk1), (bq3c, bq3), (bk3c, bk3), (gammac, gamma), (betac, beta)):
                load(dst[:], src)
            for dst, src in ((bv1B, bv1), (bo1B, bo1), (b1B, b1), (b2B, b2), (bv3B, bv3)):
                load(dst[:], src.partition_broadcast(P))

            def load_x(b):
                sp.dma_start(xn[:], x_in[bass.ds(b, 1)].rearrange("o (t p) d -> p (o t) d", p=P)).then_inc(x_in_s.sem, 16)
                sp.dma_start(mask[:], mask_in[bass.ds(b, 1)].rearrange("o p t -> p (o t)")).then_inc(x_in_s.sem, 16)

            def load_adj(b):
                sp.dma_start(adjN[:], adj_in[bass.ds(b, 1)].rearrange("o (t p) n -> p (o t) n", p=P)).then_inc(adj_in_s.sem, 16)

            def load_w1():
                for i in range(3):
                    sp.dma_start(W1[:, i], w1attn[i].rearrange("(t p) d -> p t d", p=P)).then_inc(w1_in.sem, 16)

            load_w1()
            sp.sem_inc(x_free.sem, 1)
            sp.wait_ge(setup_dve.sem, 3)
            load_x(0)
            load_adj(0)

            def batch(b, last):
                sp.wait_ge(*lo_s(b, GROUPS * NH))
                stand(sp, waited_sp)
                for dst, parts in ((kS, (khi, khi, klo, klo)), (qS, (qhi, qlo, qhi, qlo))):
                    if dst is qS:
                        sp.wait_ge(*lo_s(b, 2 * GROUPS * NH))
                        stand(sp, waited_sp)
                    for j in range(HPG):
                        done = kS_in if dst is kS else qS_in[j]
                        for r, src in enumerate(parts):
                            to = dst[HD * r:HD * r + HD].rearrange("p (g j) n -> p g j n", j=HPG)[:, :, j]
                            sp.dma_start(to.bitcast(F32), src[HD * j:HD * j + HD].bitcast(F32)).then_inc(done.sem, 16)
                sp.wait_ge(*pv_ps(b, NT * GROUPS))
                stand(sp, waited_sp)
                if not last:
                    load_w1()
                sp.dma_start(W1h[:], w1T.rearrange("(t p) d -> p t d", p=P)).then_inc(w2_in.sem, 16)
                sp.dma_start(W2g[:], w2T.rearrange("(t p) d -> p t d", p=P)).then_inc(w2_in.sem, 16)
                sp.dma_start(wB[:], adj_in[bass.ds(b, 1)][0, 0].partition_broadcast(P)).then_inc(wB_in.sem, 16)
                sp.wait_ge(*a3_ps(b, NT))
                stand(sp, waited_sp)
                for i, w in enumerate(w3attn):
                    sp.dma_start(W3[:, i], w.rearrange("(t p) d -> p t d", p=P)).then_inc(w3_in.sem, 16)
                if not last:
                    load_x(b + 1)
                    load_adj(b + 1)
                sp.wait_ge(*x3s(b, NT))
                stand(sp, waited_sp)
                sp.dma_start(out[bass.ds(b, 1)].rearrange("o (t p) d -> p (o t) d", p=P), x[:]).then_inc(out_s.sem, 16)
                sp.wait_ge(*out_s(b, 16))
                sp.sem_inc(x_free.sem, 1)

            with sp.Fori(0, B - 1) as b:
                batch(b, False)
            batch(B - 1, True)

        @block.gpsimd
        def _(pool):
            pool.memset(ident[:], 0.0).then_inc(consts_ready.sem, 1)
            pool.wait_ge(consts_ready.sem, 1)
            pool.affine_select(out=ident[:], in_=ident[:], compare_op=ALU.not_equal, fill=1.0, base=0,
                               pattern=[[-1, P]], channel_multiplier=1).then_inc(consts_ready.sem, 1)
            pool.memset(ones[:], 1.0).then_inc(consts_ready.sem, 1)
            pool.memset(mhalf[:], -0.5).then_inc(consts_ready.sem, 1)
            pool.wait_ge(consts_ready.sem, 4)

            def norm_scale(b, l):
                for s in range(NH):
                    of = slice(TPH * s, TPH * (s + 1))
                    pool.wait_ge(*mvs(b, TPH * after(l, s)))
                    stand(pool, waited_pool)
                    pool.tensor_scalar(ve[:, of], mv[:, of, 1], EPS, 1.0, ALU.add, ALU.mult).then_inc(ves.sem, 1)
                    pool.wait_ge(*ves(b, after(l, s)))
                    pool.tensor_tensor(rstd[:, of], ve[:, of], mhalf[:, of], ALU.pow).then_inc(rstds.sem, 1)

            def batch(b, last):
                norm_scale(b, 1)
                pool.wait_ge(*hs(b, 2 * NT))
                pool.tensor_tensor(x[:], x[:], bo1B[:].unsqueeze(1).broadcast_to([P, NT, D]), ALU.add).then_inc(xbo.sem, 1)
                for g in range(NT * GROUPS):
                    pool.wait_ge(*invs(b, g + 1))
                    if g:
                        pool.wait_ge(*R_ps(b, g))
                    stand(pool, waited_pool)
                    pool.tensor_scalar(rs[:], sm[:, HPG * g:HPG * g + HPG].unsqueeze(2).broadcast_to([P, HPG, HD]),
                                       1.0, None, ALU.mult).then_inc(rss.sem, 1)
                    if g % GROUPS == GROUPS - 1:
                        t = g // GROUPS
                        pool.wait_ge(*zs(b, HEADS * (t + 1)))
                        stand(pool, waited_pool)
                        pool.tensor_scalar(H[:, t], adjN[:, t], 0.0, 0.0, ALU.is_equal, ALU.is_equal).then_inc(Hs.sem, 1)
                norm_scale(b, 2)
                pool.wait_ge(*hls(b, NT))
                stand(pool, waited_pool)
                pool.tensor_scalar(h[:, :, 0:D], h[:, :, 0:D], 0.0, None, ALU.max).then_inc(xh.sem, 1)
                pool.wait_ge(*xh(b, 1))
                pool.tensor_tensor(x[:], x[:], h[:, :, 0:D], ALU.add).then_inc(xh.sem, 1)
                pool.wait_ge(*xh(b, 2))
                pool.tensor_tensor(x[:], x[:], b2B[:].unsqueeze(1).broadcast_to([P, NT, D]), ALU.add).then_inc(xhb.sem, 1)
                norm_scale(b, 3)
                pool.wait_ge(*a4_ps(b, NT))
                stand(pool, waited_pool)
                pool.memset(v3[:, :, D:HW], 1.0).then_inc(ones_col.sem, 1)
                norm_scale(b, 4)
                if not last:
                    norm_scale(b + 1, 0)

            norm_scale(0, 0)
            with pool.Fori(0, B - 1) as b:
                batch(b, False)
            batch(B - 1, True)

        @block.vector
        def _(dve):
            dve.wait_ge(weights_in.sem, 16 * NW)
            for t in range(FT):
                dve.tensor_copy(betaB[:, t], betac[:, t:t + 1].broadcast_to([P, P])).then_inc(beta_bc.sem, 1)
            dve.wait_ge(setup_pe.sem, 1)
            dve.tensor_copy(W0[:, 0, 0:D], ps[:, 0, 0:D]).then_inc(setup_dve.sem, 1)
            dve.tensor_copy(W0[:, 1, 0:D], ps[:, 1, 0:D]).then_inc(setup_dve.sem, 1)
            dve.wait_ge(setup_pe.sem, 2)
            dve.tensor_copy(cB[:], ps[:, 2, 0:D]).then_inc(setup_dve.sem, 1)

            def statistics(b, l, t, src):
                dve.bn_stats(stats[:, t], src).then_inc(stat.sem, 1)

            def aggregate(b, l, t):
                dve.wait_ge(*stat(b, NT * l + t + 1))
                stand(dve, waited_dve)
                dve.bn_aggr(mv[:, t], stats[:, t]).then_inc(mvs.sem, 1)

            def shift(b, l, s):
                of = slice(TPH * s, TPH * (s + 1))
                dve.wait_ge(*rstds(b, after(l, s)))
                dve.wait_ge(*mvs(b, TPH * after(l, s)))
                dve.scalar_tensor_tensor(nmr[:, of], mv[:, of, 0], -1.0, rstd[:, of], ALU.mult, ALU.mult).then_inc(nmrs.sem, 1)

            def norm0(b, t):
                if t == 0:
                    dve.wait_ge(*x_in_s(b, 32))
                if t < NT:
                    statistics(b, 0, t, xn[:, t])
                if 1 <= t <= NT:
                    aggregate(b, 0, t - 1)
                if t in (TPH + 2, NT + 2):
                    shift(b, 0, (t - 3) // TPH)

            def mask_h(b, t):
                dve.wait_ge(*hs(b, t + 1))
                dve.tensor_scalar(mh[:, t], h[:, t, 0:D], mask[:, t:t + 1], None, ALU.mult).then_inc(mhs.sem, 1)

            def hT_copies(b, n, s):
                for c in range(DT):
                    k = n * 2 * DT + s * DT + c
                    dve.wait_ge(*hT_ps(b, k + 1))
                    dve.tensor_copy((hT, hT1, hT)[n][:, c, half(s)], ps[:, 4 + 2 * s + c]).then_inc(hTs.sem, 1)

            def batch(b, last):
                def lower(lo, hi, t, upper_done, done):
                    dve.wait_ge(*upper_done(b, t + 1))
                    dve.scalar_tensor_tensor(lo[:, t], ps[:, bank(t), 0:D], be[:, 1, t:t + 1], hi[:, t].bitcast(F32),
                                             ALU.mult, ALU.subtract).then_inc(done.sem, 1)

                dve.tensor_scalar(mask16[:], mask[:], W_SCALE, None, ALU.mult).then_inc(chain.sem, 1)
                for n in range(1, NT * NH, 2):
                    dve.wait_ge(*aT_ps(b, n + 1))
                    jt, s = n // NH, n % NH
                    dve.tensor_copy(adjT[:, jt, half(s)], ps[:, n % 4]).then_inc(aT_dve.sem, 1)
                for s in range(NH):
                    hT_copies(b, 0, s)
                for t in range(NT):
                    dve.wait_ge(*agg_ps(b, t + 1))
                    dve.wait_ge(*gs(b, t + 1))
                    if t:
                        dve.wait_ge(*wrs(b, t))
                    dve.tensor_tensor_reduce(E3[:, 0, 0:D], ps[:, 6 + t % 2, 0:D], G[:, t], 1.0, 0.0,
                                             ALU.mult, ALU.add, sw[:, 0, t:t + 1]).then_inc(wrs.sem, 1)
                dve.wait_ge(*wrs(b, NT))
                dve.wait_ge(*chain(b, 1))
                dve.tensor_tensor(sw[:, 1], sw[:, 0], mask16[:], ALU.mult).then_inc(chain.sem, 1)
                dve.wait_ge(*chain(b, 2))
                dve.reduce_max(s1[:, 0:1], sw[:, 1], AX.X).then_inc(chain.sem, 1)
                dve.wait_ge(*chain(b, 3))
                dve.tensor_copy(E3[:, 1, 0:P], s1[:, 0:1].broadcast_to([P, P])).then_inc(wm_bc.sem, 1)
                dve.wait_ge(*wmT_ps(b, 1))
                dve.tensor_reduce(s1[:, 1:2], ps[:, 4, 0:P], AX.X, ALU.max, negate=True).then_inc(nwms.sem, 1)
                dve.wait_ge(*esum_ps(b, 1))
                dve.reciprocal(s1[:, 3:4], ps[:, 5, 0:1]).then_inc(chain.sem, 1)
                dve.wait_ge(*chain(b, 4))
                dve.tensor_scalar(sw[:, 3], sw[:, 2], s1[:, 3:4], None, ALU.mult).then_inc(chain.sem, 1)
                dve.wait_ge(*chain(b, 5))
                dve.wait_ge(*x_free(b, 1))
                for t in range(NT + 2):
                    if t < NT:
                        dve.wait_ge(*V_ps(b, t // 2 * 2 + 2))
                        dve.scalar_tensor_tensor(x[:, t], ps[:, t // 2, (t % 2) * D:(t % 2 + 1) * D], sw[:, 3, t:t + 1],
                                                 xn[:, t], ALU.mult, ALU.add).then_inc(x0s.sem, 1)
                    if 1 <= t <= NT:
                        dve.wait_ge(*x0s(b, t))
                        statistics(b, 1, t - 1, x[:, t - 1])
                    if t >= 2:
                        aggregate(b, 1, t - 2)
                    if t == TPH + 2:
                        shift(b, 1, 0)
                shift(b, 1, 1)
                def add_bv(s):
                    for t in range(TPH * s, TPH * (s + 1)):
                        dve.wait_ge(*v_ps(b, t + 1))
                        dve.tensor_tensor(v[:, t], ps[:, t % 4, 0:D], bv1B[:], ALU.add).then_inc(vs.sem, 1)

                hT_copies(b, 1, 0)
                add_bv(0)
                hT_copies(b, 1, 1)
                for n in range(2 * GROUPS * NH):
                    bias, hi, lo = ((bk1c, khi, klo), (bq1c, qhi, qlo))[n // (GROUPS * NH)]
                    g, s = n % (GROUPS * NH) // NH, n % NH
                    dve.wait_ge(*hi_s(b, n + 1))
                    dve.scalar_tensor_tensor(lo[:, g, half(s)], ps[:, 4 + n % 4], bias[:, g:g + 1],
                                             hi[:, g, half(s)].bitcast(F32), ALU.add, ALU.subtract).then_inc(lo_s.sem, 1)
                add_bv(1)

                def evacuate(u):
                    if evacuates_both(u):
                        return
                    bank = turn_bank((u, 1))
                    dve.wait_ge(*T_ps(b, 2 * u + 2))
                    if u >= PTS:
                        dve.wait_ge(*pv_ps(b, (u - PTS) // HPG + 1))
                    dve.tensor_copy(PT[:, u % PTS, NT // 2:NT], heads_of(ps[:, bank])).then_inc(PT_dve.sem, 1)

                def inverse_sums(g):
                    dve.wait_ge(*exps(b, HPG * (g + 1)))
                    dve.reciprocal(sm[:, HPG * g:HPG * g + HPG], sm[:, HPG * g:HPG * g + HPG]).then_inc(invs.sem, 1)

                def normalise(g):
                    dve.wait_ge(*pv_ps(b, g + 1))
                    if g >= GROUPS:
                        dve.wait_ge(*o_ps(b, (g - GROUPS) // GROUPS + 1))
                    dve.tensor_tensor(ctxn[:, g % GROUPS], ps[:, 7, 0:P], Rs[:], ALU.mult).then_inc(ctxs.sem, 1)

                def add_output(t):
                    dve.wait_ge(*o_ps(b, t + 1))
                    if t == 0:
                        dve.wait_ge(*xbo(b, 1))
                    dve.tensor_tensor(x[:, t], ps[:, turn_bank((t, "out")), 0:D], x[:, t], ALU.add).then_inc(x1s.sem, 1)

                for u in range(STEPS):
                    if u < UNITS:
                        dve.wait_ge(*S_ps(b, u + 1))
                        if u >= ZS:
                            dve.wait_ge(*T_ps(b, 2 * (u - ZS) + 2))
                        stand(dve, waited_dve)
                        dve.tensor_tensor_reduce(Z[:, u % ZS], ps[:, 2 * (u % 2):2 * (u % 2) + 2].rearrange("p a n -> p (a n)"),
                                                 adjN[:, u // HEADS], SCORE_SCALE, LOWEST, ALU.mult, ALU.max,
                                                 mx[:, u:u + 1]).then_inc(zs.sem, 1)
                    if (g := group_due(u, NORMALISE)) is not None:
                        normalise(g)
                    if (t := tile_due(u, ADD)) is not None:
                        add_output(t)
                    if (t := tile_due(u, ADD + 1)) is not None:
                        dve.wait_ge(*x1s(b, t + 1))
                        statistics(b, 2, t, x[:, t])
                    if (t := tile_due(u, ADD + 2)) is not None:
                        aggregate(b, 2, t)
                    if 2 <= u < UNITS + 2:
                        evacuate(u - 2)
                    if u < UNITS:
                        dve.wait_ge(*zs(b, u + 1))
                        dve.tensor_scalar(nm[:, u:u + 1], mx[:, u:u + 1], -1.0, None, ALU.mult).then_inc(nms.sem, 1)
                    if (g := group_due(u, INVERT)) is not None:
                        inverse_sums(g)

                for t in range(NT + 1):
                    if t < NT:
                        if t % TPH == 0:
                            shift(b, 2, t // TPH)
                            dve.wait_ge(*nmrs(b, after(2, t // TPH)))
                        dve.tensor_scalar(h[:, t, 0:D], x[:, t], rstd[:, t:t + 1], nmr[:, t:t + 1], ALU.mult, ALU.add).then_inc(h_d.sem, 1)
                    if t:
                        dve.wait_ge(*h_d(b, t))
                        dve.wait_ge(*hhs(b, t))
                        dve.scalar_tensor_tensor(hl[:, t - 1], h[:, t - 1, 0:D], 0.0, hh[:, t - 1, 0:D].bitcast(F32),
                                                 ALU.max, ALU.subtract).then_inc(hls.sem, 1)
                for t in range(NT):
                    dve.tensor_scalar(HT[:, t], adjT[:, t], 0.0, None, ALU.not_equal).then_inc(HTs.sem, 1)
                for t in range(NT + 1):
                    if t < NT:
                        dve.wait_ge(*a1_ps(b, t + 1))
                        dve.tensor_scalar(be[:, 0, t:t + 1], ps[:, bank(t), D:D + 1], 1.0, None, ALU.max).then_inc(be_a.sem, 1)
                        dve.wait_ge(*be_a(b, t + 1))
                        dve.reciprocal(be[:, 1, t:t + 1], be[:, 0, t:t + 1]).then_inc(be_b.sem, 1)
                    if t:
                        lower(Ul, Uh, t - 1, uhs, Us)
                dve.wait_ge(*wB_in(b, 16))
                for t in range(NT):
                    dve.wait_ge(*Hs(b, t + 1))
                    if t:
                        dve.wait_ge(*dns(b, t))
                    dve.scalar_tensor_tensor(junk[:], H[:, t].bitcast(F32), 1.0, wB[:], ALU.mult, ALU.mult,
                                             accum_out=dn[:, 0, t:t + 1]).then_inc(dns.sem, 1)
                dve.wait_ge(*dns(b, NT))
                dve.tensor_scalar(dn[:, 1], dn[:, 0], 0.0, None, ALU.is_gt).then_inc(chain.sem, 1)
                dve.tensor_scalar(dn[:, 2], dn[:, 0], TINY, None, ALU.max).then_inc(chain.sem, 1)
                dve.wait_ge(*chain(b, 7))
                dve.reciprocal(dn[:, 3], dn[:, 2]).then_inc(chain.sem, 1)
                dve.wait_ge(*chain(b, 8))
                dve.tensor_tensor(dn[:, 3], dn[:, 3], dn[:, 1], ALU.mult).then_inc(chain.sem, 1)
                dve.wait_ge(*w2_in(b, 32))
                for t in range(FT):
                    dve.tensor_scalar(W2g[:, t], W2g[:, t], gammac[:, t:t + 1], None, ALU.mult).then_inc(w2g_s.sem, 1)
                dve.wait_ge(*chain(b, 9))
                for t in range(NT + 1):
                    if t < NT:
                        dve.wait_ge(*y_ps(b, t + 1))
                        dve.scalar_tensor_tensor(h2[:, t], ps[:, t % 4], dn[:, 3, t:t + 1], b1B[:], ALU.mult,
                                                 ALU.add).then_inc(ys.sem, 1)
                    if t:
                        dve.wait_ge(*yrelu(b, t))
                        statistics(b, 3, t - 1, h2[:, t - 1])
                        aggregate(b, 3, t - 1)
                    if t and t % TPH == 0:
                        shift(b, 3, t // TPH - 1)
                for s in range(NH):
                    for f in range(FT):
                        n = FT * s + f
                        dve.wait_ge(*h2T_ps(b, n + 1))
                        dve.tensor_copy(h2T[:, f, half(s)], ps[:, 4 + n % 4]).then_inc(h2Ts.sem, 1)
                    if s == 0:
                        dve.wait_ge(*xh(b, 2))
                    for t in range(TPH * s, TPH * (s + 1)):
                        dve.wait_ge(*x2_ps(b, t + 1))
                        dve.tensor_tensor(h[:, t, 0:D], ps[:, t % 4, 0:D], cB[:], ALU.add).then_inc(x2t.sem, 1)
                        dve.wait_ge(*x2h(b, t + 1))
                        dve.tensor_tensor(Ul[:, t], h[:, t, 0:D], Uh[:, t].bitcast(F32), ALU.subtract).then_inc(x2s.sem, 1)
                for t in range(NT):
                    dve.wait_ge(*a3_ps(b, t + 1))
                    lower(Vl, Vh, t, vhs, v2s)
                dve.wait_ge(*xhb(b, 1))
                for t in range(NT + 2):
                    if t < NT:
                        dve.wait_ge(*a4_ps(b, t + 1))
                        dve.scalar_tensor_tensor(x[:, t], ps[:, bank(t), 0:D], dn[:, 3, t:t + 1], x[:, t], ALU.mult,
                                                 ALU.add).then_inc(x2f.sem, 1)
                    if 1 <= t <= NT:
                        dve.wait_ge(*x2f(b, t))
                        statistics(b, 4, t - 1, x[:, t - 1])
                    if t >= 2:
                        aggregate(b, 4, t - 2)
                    if t == TPH + 3:
                        shift(b, 4, 0)
                shift(b, 4, 1)
                for s in range(NH):
                    hT_copies(b, 2, s)
                for t in range(NT):
                    dve.wait_ge(*v3_ps(b, t + 1))
                    if t == 0:
                        dve.wait_ge(*ones_col(b, 1))
                    dve.tensor_tensor(v3[:, t, 0:D], ps[:, 4 + t % 4, 0:D], bv3B[:], ALU.add).then_inc(v3s.sem, 1)

                def mask_exp(n):
                    s, kt = n // NT, n % NT
                    dve.wait_ge(*e3s(b, n + 1))
                    dve.tensor_tensor(P3[:, s, kt], E3[:, n % 2], adjT[:, kt, half(s)], ALU.mult).then_inc(p3s.sem, 1)

                def finish(t):
                    dve.wait_ge(*o3_ps(b, t + 1))
                    dve.reciprocal(rden[:, t:t + 1], ps[:, 4 + t % 2, D:D + 1]).then_inc(rd3.sem, 1)
                    dve.wait_ge(*rd3(b, t + 1))
                    dve.scalar_tensor_tensor(x[:, t], ps[:, 4 + t % 2, 0:D], rden[:, t:t + 1], x[:, t], ALU.mult,
                                             ALU.add).then_inc(x3s.sem, 1)

                for n in range(NH * NT):
                    mask_exp(n)
                    if not last and n >= 4:
                        norm0(b + 1, n - 4)
                for t in range(NT):
                    finish(t)
                    if not last:
                        mask_h(b + 1, t)

            for t in range(NT + 3):
                norm0(0, t)
            for t in range(NT):
                mask_h(0, t)
            with dve.Fori(0, B - 1) as b:
                batch(b, False)
            batch(B - 1, True)

        @block.scalar
        def _(act):
            def normalise(b, l, k, src):
                for t in range(NT):
                    if t % TPH == 0:
                        act.wait_ge(*nmrs(b, after(l, t // TPH)))
                    act.activation(h[:, t, 0:D], src[:, t], ACT.Relu, bias=nmr[:, t:t + 1],
                                   scale=rstd[:, t:t + 1]).then_inc(hs.sem, 1)

            def batch(b, last):
                for n in range(0, NT * NH, 2):
                    act.wait_ge(*aT_ps(b, n + 1))
                    jt, s = n // NH, n % NH
                    act.activation(adjT[:, jt, half(s)], ps[:, n % 4], ACT.Copy).then_inc(aT_act.sem, 1)
                for t in range(NT):
                    act.wait_ge(*g_ps(b, t + 1))
                    act.activation(G[:, t], ps[:, 4 + t % 2, 0:D], ACT.Copy).then_inc(gs.sem, 1)
                act.wait_ge(*nwms(b, 1))
                act.activation(sw[:, 2], sw[:, 1], ACT.Exp, bias=s1[:, 1:2], accum_out=s1[:, 2:3]).then_inc(es.sem, 1)
                normalise(b, 1, 1, x)
                for n in range(2 * GROUPS * NH):
                    bias, hi = ((bk1c, khi), (bq1c, qhi))[n // (GROUPS * NH)]
                    g, s = n % (GROUPS * NH) // NH, n % NH
                    act.wait_ge(*kq_ps(b, n + 1))
                    act.activation(hi[:, g, half(s)], ps[:, 4 + n % 4], ACT.Identity, bias=bias[:, g:g + 1]).then_inc(hi_s.sem, 1)

                def evacuate(u):
                    for half_of_u in range(1 + evacuates_both(u)):
                        bank = turn_bank((u, half_of_u))
                        act.wait_ge(*T_ps(b, 2 * u + half_of_u + 1))
                        if u >= PTS:
                            act.wait_ge(*pv_ps(b, (u - PTS) // HPG + 1))
                        first = NT // 2 * half_of_u
                        act.activation(PT[:, u % PTS, first:first + NT // 2], heads_of(ps[:, bank]), ACT.Copy).then_inc(PT_act.sem, 1)

                for u in range(STEPS):
                    if (g := group_due(u, COPY)) is not None:
                        act.wait_ge(*R_ps(b, g + 1))
                        act.activation(Rs[:], ps[:, 7, P:2 * P], ACT.Copy).then_inc(Rss.sem, 1)
                    if u < UNITS:
                        act.wait_ge(*nms(b, u + 1))
                        act.activation(Z[:, u % ZS], Z[:, u % ZS], ACT.Exp, bias=nm[:, u:u + 1],
                                       accum_out=sm[:, u:u + 1]).then_inc(exps.sem, 1)
                    if 1 <= u < UNITS + 1:
                        evacuate(u - 1)
                act.wait_ge(*x1s(b, NT))
                act.activation(hh[:, :, D:HW], ones[:, 0:2 * NT].rearrange("p (t c) -> p t c", c=2), ACT.Copy).then_inc(ones_h.sem, 1)
                for t in range(NT):
                    if t % TPH == 0:
                        act.wait_ge(*nmrs(b, after(2, t // TPH)))
                    act.activation(hh[:, t, 0:D], x[:, t], ACT.Relu, bias=nmr[:, t:t + 1], scale=rstd[:, t:t + 1]).then_inc(hhs.sem, 1)
                for t in range(NT):
                    act.wait_ge(*be_b(b, t + 1))
                    act.activation(Uh[:, t], ps[:, bank(t), 0:D], ACT.Copy, scale=be[:, 1, t:t + 1]).then_inc(uhs.sem, 1)
                for n in range(DT * NH):
                    act.wait_ge(*a2_ps(b, n + 1))
                    act.activation(A2T[:, n % DT, half(n // DT)], ps[:, 4 + n], ACT.Copy).then_inc(a2s.sem, 1)

                def norm2(t):
                    if t % TPH == 0:
                        act.wait_ge(*nmrs(b, after(3, t // TPH)))
                    act.activation(h2[:, t], h2[:, t], ACT.Identity, bias=nmr[:, t:t + 1],
                                   scale=rstd[:, t:t + 1]).then_inc(h2s.sem, 1)

                for t in range(NT):
                    act.wait_ge(*ys(b, t + 1))
                    act.activation(h2[:, t], h2[:, t], ACT.Relu).then_inc(yrelu.sem, 1)
                    if t >= TPH + 2:
                        norm2(2 * (t - TPH - 2))
                        norm2(2 * (t - TPH - 2) + 1)
                for t in range(TPH, NT):
                    norm2(t)
                for t in range(NT):
                    act.wait_ge(*x2t(b, t + 1))
                    act.activation(Uh[:, t], h[:, t, 0:D], ACT.Copy).then_inc(x2h.sem, 1)
                for t in range(NT):
                    act.wait_ge(*a3_ps(b, t + 1))
                    act.activation(Vh[:, t], ps[:, bank(t), 0:D], ACT.Copy, scale=be[:, 1, t:t + 1]).then_inc(vhs.sem, 1)
                normalise(b, 4, 2, x)
                for n in range(2 * DT * NH):
                    s, w, f = n // (2 * DT), n // DT % 2, n % DT
                    bias, dst = ((bk3c, k3T), (bq3c, q3T))[w]
                    act.wait_ge(*qk3_ps(b, n + 1))
                    act.activation(dst[:, f, half(s)], ps[:, n % 4], ACT.Identity, bias=bias[:, f:f + 1]).then_inc(qk3s.sem, 1)
                for n in range(NH * NT):
                    act.wait_ge(*s3_ps(b, n + 1))
                    if n >= 2:
                        act.wait_ge(*p3s(b, n - 1))
                    act.activation(E3[:, n % 2], ps[:, n % 4], ACT.Exp).then_inc(e3s.sem, 1)

                if not last:
                    normalise(b + 1, 0, 0, xn)

            normalise(0, 0, 0, xn)
            with act.Fori(0, B - 1) as b:
                batch(b, False)
            batch(B - 1, True)

        @block.tensor
        def _(pe):
            def product(dst, pairs):
                for i, (lhsT, rhs) in enumerate(pairs):
                    mm = pe.matmul(dst, lhsT, rhs, start=(i == 0), stop=(i == len(pairs) - 1))
                return mm

            pe.wait_ge(weights_in.sem, 16 * NW)
            for a in range(DT):
                mm = product(ps[:, a, 0:D], [(wqk0s[:, c, rows(a)], wqk0s[:, DT + c]) for c in range(DT)])
            mm.then_inc(setup_pe.sem, 1)
            pe.wait_ge(consts_ready.sem, 4)
            pe.wait_ge(beta_bc.sem, FT)
            product(ps[:, 2, 0:D], [(betaB[:, t], W2g[:, t]) for t in range(FT)]).then_inc(setup_pe.sem, 1)
            pe.wait_ge(setup_dve.sem, 3)

            def transpose_h(b, k, s):
                for c in range(DT):
                    for a in range(TPH):
                        t = TPH * s + a
                        pe.wait_ge(*hs(b, NT * k + t + 1))
                        mm = pe.transpose(ps[:, 4 + 2 * s + c, rows(a)], h[:, t, rows(c)], ident[:])
                    mm.then_inc(hT_ps.sem, 1)

            def batch(b):
                pe.wait_ge(*adj_in_s(b, 16))
                for n in range(NT * NH):
                    jt, s = n // NH, n % NH
                    if n >= 4:
                        done = aT_act if n % 2 == 0 else aT_dve
                        pe.wait_ge(*done(b, (n - 4) // 2 + 1))
                    for a in range(TPH):
                        mm = pe.transpose(ps[:, n % 4, rows(a)], adjN[:, TPH * s + a, rows(jt)], ident[:])
                    mm.then_inc(aT_ps.sem, 1)
                for s in range(NH):
                    transpose_h(b, 0, s)
                pe.wait_ge(*hTs(b, 2 * DT))
                for t in range(NT):
                    if t >= 2:
                        pe.wait_ge(*gs(b, t - 1))
                    product(ps[:, 4 + t % 2, 0:D], [(hT[:, c, rows(t)], W0[:, c, 0:D]) for c in range(DT)]).then_inc(g_ps.sem, 1)
                pe.wait_ge(*mhs(b, NT))
                pe.wait_ge(*aT_act(b, NT * NH // 2))
                pe.wait_ge(*aT_dve(b, NT * NH // 2))
                for t in range(NT):
                    if t >= 2:
                        pe.wait_ge(*wrs(b, t - 1))
                    product(ps[:, 6 + t % 2, 0:D], [(adjT[:, j, rows(t)], mh[:, j]) for j in range(NT)]).then_inc(agg_ps.sem, 1)
                def values(t):
                    product(ps[:, t // 2, (t % 2) * D:(t % 2 + 1) * D],
                            [(hT[:, c, rows(t)], W0[:, c, D:2 * D]) for c in range(DT)]).then_inc(V_ps.sem, 1)

                values(0)
                pe.wait_ge(*wm_bc(b, 1))
                pe.wait_ge(*gs(b, NT))
                pe.transpose(ps[:, 4, 0:P], E3[:, 1, 0:P], ident[:]).then_inc(wmT_ps.sem, 1)
                values(1)
                pe.wait_ge(*es(b, 1))
                pe.matmul(ps[:, 5, 0:1], ones[:], s1[:, 2:3], start=True, stop=True).then_inc(esum_ps.sem, 1)
                for t in range(2, NT):
                    values(t)
                def project_v(s):
                    for t in range(TPH * s, TPH * (s + 1)):
                        if t >= 4:
                            pe.wait_ge(*vs(b, t - 3))
                        product(ps[:, t % 4, 0:D], [(hT1[:, c, rows(t)], Wv1[:, c]) for c in range(DT)]).then_inc(v_ps.sem, 1)

                transpose_h(b, 1, 0)
                pe.wait_ge(*hTs(b, 3 * DT))
                pe.wait_ge(*x0s(b, NT))
                pe.wait_ge(*w1_in(b, 48))
                project_v(0)
                transpose_h(b, 1, 1)
                pe.wait_ge(*hTs(b, 4 * DT))
                for n in range(2 * GROUPS * NH):
                    w = (Wk1, Wq1)[n // (GROUPS * NH)]
                    g, s = n % (GROUPS * NH) // NH, n % NH
                    if n >= 4:
                        pe.wait_ge(*lo_s(b, n - 3))
                    product(ps[:, 4 + n % 4], [(w[:, c, rows(g)], hT1[:, c, half(s)]) for c in range(DT)]).then_inc(kq_ps.sem, 1)

                project_v(1)

                def scores(u):
                    t, hd = u // HEADS, u % HEADS
                    if u >= 2:
                        pe.wait_ge(*zs(b, u - 1))
                    if u < HPG:
                        pe.wait_ge(*qS_in[u](b, 64))
                    for s in range(NH):
                        mm = pe.matmul(ps[:, 2 * (u % 2) + s], qS[:, hd, rows(t)], kS[:, hd, half(s)], start=True, stop=True)
                    mm.then_inc(S_ps.sem, 1)

                def wait_bank(use):
                    if turns.index(use) < TBANKS:
                        return
                    n, what = turns[turns.index(use) - TBANKS]
                    if what == "out":
                        pe.wait_ge(*x1s(b, n + 1))
                    elif what == 0 or evacuates_both(n):
                        pe.wait_ge(*PT_act(b, by_act(n) - (what == 0 and evacuates_both(n))))
                    else:
                        pe.wait_ge(*PT_dve(b, by_dve(n)))

                def transposes(u):
                    pe.wait_ge(*exps(b, u + 1))
                    for s in range(2):
                        wait_bank((u, s))
                        for a in range(NT // 2):
                            mm = pe.transpose(ps[:, turn_bank((u, s)), rows(a)], Z[:, u % ZS, rows(NT // 2 * s + a)], ident[:])
                        mm.then_inc(T_ps.sem, 1)

                def spread_inverses(g):
                    pe.wait_ge(*rss(b, g + 1))
                    if g:
                        pe.wait_ge(*ctxs(b, g))
                    pe.matmul(ps[:, 7, P:2 * P], rs[:].rearrange("p h d -> p (h d)"),
                              ident[:], start=True, stop=True).then_inc(R_ps.sem, 1)

                def weighted_values(g, part):
                    if part == 0:
                        pe.wait_ge(*PT_act(b, by_act(HPG * g + HPG - 1)))
                        pe.wait_ge(*PT_dve(b, by_dve(HPG * g + HPG - 1)))
                        pe.wait_ge(*Rss(b, g + 1))
                    for kt in range(sum(PARTS[:part]), sum(PARTS[:part + 1])):
                        for j in range(HPG):
                            hd = HPG * (g % GROUPS) + j
                            mm = pe.matmul(ps[HD * j:HD * j + HD, 7, 0:P],
                                           v[:, kt, HD * hd:HD * hd + HD], PT[:, (HPG * g + j) % PTS, kt],
                                           start=(kt == 0), stop=(kt == NT - 1))
                    if part == len(PARTS) - 1:
                        mm.then_inc(pv_ps.sem, 1)

                def project(t):
                    pe.wait_ge(*ctxs(b, GROUPS * (t + 1)))
                    wait_bank((t, "out"))
                    product(ps[:, turn_bank((t, "out")), 0:D], [(ctxn[:, g], Wo1[:, g]) for g in range(GROUPS)]).then_inc(o_ps.sem, 1)

                pe.wait_ge(*kS_in(b, 256))
                pe.wait_ge(*lo_s(b, 2 * GROUPS * NH))
                pe.wait_ge(*vs(b, NT))
                scores(0)
                scores(1)
                for u in range(STEPS):
                    if (t := tile_due(u, PROJECT)) is not None:
                        project(t)
                    if u + 2 < UNITS:
                        scores(u + 2)
                    for part in range(len(PARTS)):
                        if (g := group_due(u, WEIGH + part)) is not None:
                            weighted_values(g, part)
                    if u < UNITS:
                        transposes(u)
                    if (g := group_due(u, SPREAD)) is not None:
                        spread_inverses(g)
                def sum_up(dst, lhs, rhs, ready, bank_free, done):
                    TAIL = 2
                    def step(n, j):
                        for i in ((0, 1) if j == 0 else (1, 0)):
                            mm = pe.matmul(dst(n, i), lhs(n, j, i), rhs(n, j, i), start=(j == 0 and i == 0),
                                           stop=(j == NT - 1 and i == 0))
                        return mm
                    count = len(bank_free)
                    for j in range(NT - TAIL):
                        for wait in ready:
                            pe.wait_ge(*wait(b, j + 1))
                        for n in range(count):
                            if j == 0 and bank_free[n] is not None:
                                pe.wait_ge(*bank_free[n])
                            step(n, j)
                    for n in range(count):
                        for j in range(NT - TAIL, NT):
                            if n == 0:
                                for wait in ready:
                                    pe.wait_ge(*wait(b, j + 1))
                            mm = step(n, j)
                        mm.then_inc(done.sem, 1)

                def of_edges(hi, lo, width):
                    return (lambda t, i: ps[:, bank(t), 0:(D, width)[i == 0]], lambda t, j, i: H[:, j, rows(t)],
                            lambda t, j, i: (hi, lo)[i][:, j])

                def of_nodes(hi, lo):
                    return (lambda t, i: ps[:, bank(t), 0:D], lambda t, j, i: HT[:, j, rows(t)],
                            lambda t, j, i: (hi, lo)[i][:, j])

                pe.wait_ge(*ones_h(b, 1))
                sum_up(*of_edges(hh, hl, HW), (Hs, hhs, hls), [None] * NT, a1_ps)
                sum_up(lambda n, i: ps[:, 4 + n], lambda n, j, i: (Uh, Ul)[i][:, j, rows(n % DT)],
                       lambda n, j, i: HT[:, j, half(n // DT)], (HTs, Us), [Us(b, n + 1) for n in range(DT * NH)], a2_ps)
                pe.wait_ge(*w2_in(b, 32))
                for t in range(NT):
                    if t % TPH == 0:
                        pe.wait_ge(*a2s(b, DT * (t // TPH + 1)))
                    if t >= 4:
                        pe.wait_ge(*ys(b, t - 3))
                    product(ps[:, t % 4], [(A2T[:, c, rows(t)], W1h[:, c]) for c in range(DT)]).then_inc(y_ps.sem, 1)
                pe.wait_ge(*a2s(b, DT * NH))
                pe.wait_ge(*w2g_s(b, FT))
                for s in range(NH):
                    for f in range(FT):
                        n = FT * s + f
                        if n >= 4:
                            pe.wait_ge(*h2Ts(b, n - 3))
                        for a in range(TPH):
                            if f == 0:
                                pe.wait_ge(*h2s(b, TPH * s + a + 1))
                            mm = pe.transpose(ps[:, 4 + n % 4, rows(a)], h2[:, TPH * s + a, rows(f)], ident[:])
                        mm.then_inc(h2T_ps.sem, 1)
                    pe.wait_ge(*h2Ts(b, FT * (s + 1)))
                    for t in range(TPH * s, TPH * (s + 1)):
                        if s == 0:
                            pe.wait_ge(*ys(b, TPH + t + 1))
                        else:
                            pe.wait_ge(*x2t(b, t - 3))
                        product(ps[:, t % 4, 0:D], [(h2T[:, f, rows(t)], W2g[:, f]) for f in range(FT)]).then_inc(x2_ps.sem, 1)
                sum_up(*of_edges(Uh, Ul, D), (x2s,), [None] * 4 + [x2t(b, t + 1) for t in range(4, NT)], a3_ps)
                sum_up(*of_nodes(Vh, Vl), (v2s,), [v2s(b, t + 1) for t in range(NT)], a4_ps)
                for s in range(NH):
                    transpose_h(b, 2, s)
                pe.wait_ge(*w3_in(b, 48))
                pe.wait_ge(*x2f(b, NT))
                for n in range(2 * DT * NH):
                    s, w, f = n // (2 * DT), 1 - n // DT % 2, n % DT
                    pe.wait_ge(*hTs(b, 4 * DT + DT * (s + 1)))
                    if n >= 4:
                        pe.wait_ge(*qk3s(b, n - 3))
                    product(ps[:, n % 4], [(W3[:, w, c, rows(f)], hT[:, c, half(s)]) for c in range(DT)]).then_inc(qk3_ps.sem, 1)
                for t in range(NT):
                    if t >= 4:
                        pe.wait_ge(*v3s(b, t - 3))
                    product(ps[:, 4 + t % 4, 0:D], [(hT[:, c, rows(t)], W3[:, 2, c]) for c in range(DT)]).then_inc(v3_ps.sem, 1)
                pe.wait_ge(*qk3s(b, 2 * DT * NH))
                for n in range(NH * NT):
                    s, kt = n // NT, n % NT
                    if n >= 4:
                        pe.wait_ge(*e3s(b, n - 3))
                    product(ps[:, n % 4], [(k3T[:, c, rows(kt)], q3T[:, c, half(s)]) for c in range(DT)]).then_inc(s3_ps.sem, 1)
                pe.wait_ge(*v3s(b, NT))
                for t in range(NT):
                    s, a = t // TPH, t % TPH
                    pe.wait_ge(*p3s(b, NT * (s + 1)))
                    if t >= 2:
                        pe.wait_ge(*x3s(b, t - 1))
                    product(ps[:, 4 + t % 2, 0:D + 1], [(P3[:, s, j, rows(a)], v3[:, j, 0:D + 1]) for j in range(NT)]).then_inc(o3_ps.sem, 1)

            with pe.Fori(0, B) as b:
                batch(b)


def kernel(x, adj, nodemask, L0_gnn_Wqk, L0_gnn_Wv, L1_gnn_Wq, L1_gnn_bq, L1_gnn_Wk, L1_gnn_bk, L1_gnn_Wv,
           L1_gnn_bv, L1_gnn_Wo, L1_gnn_bo, L2_gnn_W1, L2_gnn_b1, L2_gnn_gamma, L2_gnn_beta, L2_gnn_W2, L2_gnn_b2,
           L3_gnn_Wq_w, L3_gnn_Wq_b, L3_gnn_Wk_w, L3_gnn_Wk_b, L3_gnn_Wv_w, L3_gnn_Wv_b):
    import numpy as np
    import concourse.bacc as bacc
    from concourse.bass_utils import run_bass_kernel_spmd

    def T(a):
        return np.ascontiguousarray(np.asarray(a).T)

    def columns(a):
        a = np.asarray(a)
        return np.swapaxes(a.reshape(*a.shape[:-1], -1, P), -1, -2)

    arrays = {
        "x_in": x, "adj_in": adj, "mask_in": columns(nodemask), "wqkT0": T(L0_gnn_Wqk), "wv0": L0_gnn_Wv,
        "wq1": T(L1_gnn_Wq), "wk1": T(L1_gnn_Wk), "wv1": T(L1_gnn_Wv), "wo1": T(L1_gnn_Wo),
        "bq1": columns(L1_gnn_bq), "bk1": columns(L1_gnn_bk), "bv1": L1_gnn_bv, "bo1": L1_gnn_bo,
        "w1T": T(L2_gnn_W1), "b1": L2_gnn_b1, "gamma": columns(L2_gnn_gamma), "beta": columns(L2_gnn_beta),
        "w2T": T(L2_gnn_W2), "b2": L2_gnn_b2,
        "wq3": T(L3_gnn_Wq_w), "wk3": T(L3_gnn_Wk_w), "wv3": T(L3_gnn_Wv_w),
        "bq3": columns(L3_gnn_Wq_b), "bk3": columns(L3_gnn_Wk_b), "bv3": L3_gnn_Wv_b,
    }
    arrays = {n: np.ascontiguousarray(a) for n, a in arrays.items()}
    nc = bacc.Bacc("TRN2", target_bir_lowering=False, num_devices=1)
    t = {n: nc.dram_tensor(n, a.shape, mybir.dt.from_np(a.dtype), kind="ExternalInput").ap() for n, a in arrays.items()}
    out = nc.dram_tensor("out", arrays["x_in"].shape, F32, kind="ExternalOutput").ap()
    build_program(nc, t["x_in"], t["adj_in"], t["mask_in"], t["wqkT0"], t["wv0"],
                  [t["wq1"], t["wk1"], t["wv1"], t["wo1"]], t["bq1"], t["bk1"], t["bv1"], t["bo1"],
                  t["w1T"], t["b1"], t["gamma"], t["beta"], t["w2T"], t["b2"],
                  [t["wq3"], t["wk3"], t["wv3"]], t["bq3"], t["bk3"], t["bv3"], out)
    r = run_bass_kernel_spmd(nc, [arrays], core_ids=[0])
    return r.results[0]["out"]
```

```python
from contextlib import ExitStack

import concourse.bass as bass
from concourse import mybir

F32 = mybir.dt.float32
F32R = mybir.dt.float32r
ALU = mybir.AluOpType
ACT = mybir.ActivationFunctionType
AX = mybir.AxisListType

P = 128
HALF = 512
EPS = 1e-5
LOWEST = -3.0e38
TINY = 1.2e-38


class Signal:

    def __init__(self, sem, per):
        self.sem, self.per = sem, per

    def __call__(self, b, n):
        return self.sem, b * self.per + n


def build_program(nc, x_in, adj_in, mask_in, wqkT0, wv0, w1attn, bq1, bk1, bv1, bo1,
                  w1T, b1, gamma, beta, w2T, b2, w3attn, bq3, bk3, bv3, out):
    B, N, D = x_in.shape
    NT = N // P
    DT = D // P
    NH = N // HALF
    TPH = HALF // P
    HID = w1T.shape[1]
    FT = HID // P
    HEADS = 8
    HD = D // HEADS
    HPG = P // HD
    GROUPS = HEADS // HPG
    UNITS = NT * HEADS
    BOTH = 4
    PTS = 8
    ZS = 3
    SCORE_SCALE = 2.0 * float(HD) ** -0.5
    W_SCALE = 1.0 / float(D) ** 0.5

    ctx = ExitStack()
    with ctx:
        def sb(name, shape, dt=F32, scope=ctx):
            return scope.enter_context(nc.sbuf_tensor(name, shape, dt))

        def signal(name, per):
            return Signal(ctx.enter_context(nc.semaphore(name)), per)

        adjT = sb("adjT", [P, NT, N])
        x = sb("x", [P, NT, D])
        ident = sb("ident", [P, P])
        ones = sb("ones", [P, P])
        W0 = sb("W0", [P, DT, 2 * D])
        Wo1 = sb("Wo1", [P, DT, D])
        bq1c = sb("bq1c", [P, DT])
        bk1c = sb("bk1c", [P, DT])
        bq3c = sb("bq3c", [P, DT])
        bk3c = sb("bk3c", [P, DT])
        gammac = sb("gammac", [P, FT])
        betac = sb("betac", [P, FT])
        bv1B = sb("bv1B", [P, D])
        bo1B = sb("bo1B", [P, D])
        pick = sb("pick", [P, 4, P], F32R)
        b2B = sb("b2B", [P, D])
        bv3B = sb("bv3B", [P, D])
        cB = sb("cB", [P, D])
        mhalf = sb("mhalf", [P, NT])
        mask = sb("mask", [P, NT])
        mask16 = sb("mask16", [P, NT])
        stats = sb("stats", [P, NT, 6])
        mv = sb("mv", [P, NT, 2])
        ve = sb("ve", [P, NT])
        rstd = sb("rstd", [P, NT])
        nmr = sb("nmr", [P, NT])
        sw = sb("sw", [P, 4, NT])
        s1 = sb("s1", [P, 8])
        nm = sb("nm", [P, UNITS])
        sm = sb("sm", [P, UNITS])
        rs = sb("rs", [P, HPG, HD])
        Rs = sb("Rs", [P, P])
        ctxn = sb("ctxn", [P, GROUPS, P])
        dn = sb("dn", [P, 4, NT])
        be = sb("be", [P, 2, NT])
        rden = sb("rden", [P, NT])
        fold = sb("fold", [P, 2 * DT + 1])
        cj = sb("cj", [P, NT])

        def region(*layouts):
            got = []
            for i, layout in enumerate(layouts):
                with ExitStack() as scope:
                    got.append([sb(n if i == 0 else f"{n}_{i}", s, d, scope) for n, s, d in layout])
            sizes = [sum(_bytes(s) for _, s, _ in layout) for layout in layouts]
            sb(f"region_{layouts[0][0][0]}", [P, max(sizes) // 4])
            return got

        def _bytes(shape):
            n = 4
            for s in shape[1:]:
                n *= s
            return n

        (adj0, adj2) = region([("adjN", [P, NT, N], F32)],
                              [("H", [P, NT, N], F32R)])
        (adjN,), (H,) = adj0, adj2
        HW = D + 2
        common = [("h", [P, NT, HW], F32), ("hT", [P, DT, N], F32)]
        (a0, a1, a2, a3, asetup) = region(
            common + [("mh", [P, NT, D], F32), ("G", [P, NT, D], F32)],
            [("qS", [P, HEADS, N], F32R), ("kS", [P, HEADS, N], F32R)],
            common[:1] + [("HT", [P, NT, N], F32R), ("Uh", [P, NT, D], F32R), ("Ul", [P, NT, D], F32R),
                          ("A2T", [P, DT, N], F32)],
            common + [("t3T", [P, DT, N], F32), ("v3", [P, NT, HW], F32), ("room", [P, DT, N], F32),
                      ("W3", [P, 2, DT, D], F32), ("W3v", [P, DT, HW], F32), ("M3", [P, DT, D], F32)],
            [("wqk0s", [P, 4, D], F32), ("betaB", [P, FT, P], F32), ("w3s", [P, 2, DT, D], F32), ("bqk", [P, DT], F32)],
        )
        h, hT, mh, G = a0
        qS, kS = a1
        _, HT, Uh, Ul, A2T = a2
        _, _, t3T, v3, _, W3, W3v, M3 = a3
        wqk0s, betaB, w3s, bqk = asetup
        (p1a, p1b, p2, p2a, p2v, p3, p2c) = region(
            [("khi", [P, GROUPS, N], F32R), ("klo", [P, GROUPS, N], F32R),
             ("qhi", [P, GROUPS, N], F32R), ("qlo", [P, GROUPS, N], F32R), ("hT1", [P, DT, N], F32),
             ("W1", [P, 3, DT, D], F32)],
            [("PT", [P, PTS, NT, P], F32), ("Z", [P, ZS, N], F32)],
            [("h2", [P, NT, HID], F32), ("h2T", [P, FT, N], F32)],
            [("hh", [P, NT, HW], F32R), ("hl", [P, NT, D], F32R), ("wB", [P, N], F32), ("junk", [P, N], F32)],
            [("Vh", [P, NT, D], F32R), ("Vl", [P, NT, D], F32R)],
            [("P3", [P, NH, NT, HALF], F32), ("E3", [P, 2, HALF], F32)],
            [("padc", [P, NH, NT, HALF], F32), ("cs", [P, D], F32), ("shiftB", [P, 2, D], F32),
             ("b1B", [P, HID], F32)],
        )
        khi, klo, qhi, qlo, hT1, W1 = p1a
        PT, Z = p1b
        h2, h2T = p2
        hh, hl, wB, junk = p2a
        Vh, Vl = p2v
        P3, E3 = p3
        _, cs, shiftB, b1B = p2c
        (r1, r2, r3) = region(
            [("v", [P, NT, D], F32)],
            [("W1h", [P, DT, HID], F32), ("W2g", [P, FT, D], F32)],
            [("xn", [P, NT, D], F32)],
        )
        (v,), (W1h, W2g), (xn,) = r1, r2, r3
        Wq1, Wk1, Wv1 = (W1[:, i] for i in range(3))

        ps = ctx.enter_context(nc.psum_tensor("ps", [P, 8, HALF], F32))

        weights_in = signal("weights_in", 0)
        consts_ready = signal("consts_ready", 0)
        beta_bc = signal("beta_bc", 0)
        setup_pe = signal("setup_pe", 0)
        setup_dve = signal("setup_dve", 0)
        picks = signal("picks", 0)
        waited_dve = signal("waited_dve", 0)
        waited_pool = signal("waited_pool", 0)
        waited_sp = signal("waited_sp", 0)
        adj_in_s = signal("adj_in_s", 16)
        x_in_s = signal("x_in_s", 32)
        out_s = signal("out_s", 16)
        x_free = signal("x_free", 1)
        kS_in = signal("kS_in", 64 * (HPG - 1))
        qS_in = [signal(f"qS_in{j}", 64) for j in range(HPG - 1)]
        last_ps = signal("last_ps", 2 * GROUPS * NH)
        lasts = signal("lasts", 2 * GROUPS * NH)
        w2_in = signal("w2_in", 48)
        wB_in = signal("wB_in", 16)
        w3_in = signal("w3_in", 48)
        w1_in = signal("w1_in", 48)
        stat = signal("stat", 5 * NT)
        mvs = signal("mvs", 5 * NT)
        ves = signal("ves", 5 * NH)
        rstds = signal("rstds", 5 * NH)
        nmrs = signal("nmrs", 5 * NH)
        hs = signal("hs", 3 * NT)
        hT_ps = signal("hT_ps", 3 * 2 * DT)
        hTs = signal("hTs", 3 * 2 * DT)
        aT_ps = signal("aT_ps", NT * NH)
        aT_act = signal("aT_act", NT * NH // 2)
        aT_dve = signal("aT_dve", NT * NH // 2)
        g_ps = signal("g_ps", NT)
        gs = signal("gs", NT)
        mhs = signal("mhs", NT)
        agg_ps = signal("agg_ps", NT)
        wrs = signal("wrs", NT)
        chain = signal("chain", 9)
        wm_bc = signal("wm_bc", 1)
        wmT_ps = signal("wmT_ps", 1)
        nwms = signal("nwms", 1)
        es = signal("es", 1)
        esum_ps = signal("esum_ps", 1)
        V_ps = signal("V_ps", NT)
        x0s = signal("x0s", NT)
        xbo = signal("xbo", 1)
        v_ps = signal("v_ps", NT)
        vs = signal("vs", NT)
        kq_ps = signal("kq_ps", 2 * GROUPS * NH)
        hi_s = signal("hi_s", 2 * GROUPS * NH)
        lo_s = signal("lo_s", 2 * GROUPS * NH)
        S_ps = signal("S_ps", UNITS)
        zs = signal("zs", UNITS)
        nms = signal("nms", UNITS)
        exps = signal("exps", UNITS)
        T_ps = signal("T_ps", 2 * UNITS)
        PT_act = signal("PT_act", UNITS + UNITS // BOTH)
        PT_dve = signal("PT_dve", UNITS - UNITS // BOTH)
        pv_ps = signal("pv_ps", NT * GROUPS)
        R_ps = signal("R_ps", NT * GROUPS)
        invs = signal("invs", NT * GROUPS)
        rss = signal("rss", NT * GROUPS)
        Rss = signal("Rss", NT * GROUPS)
        ctxs = signal("ctxs", NT * GROUPS)
        o_ps = signal("o_ps", NT)
        x1s = signal("x1s", NT)
        ones_col = signal("ones_col", 1)
        ones_h = signal("ones_h", 1)
        h_d = signal("h_d", NT)
        hhs = signal("hhs", NT)
        hls = signal("hls", NT)
        uhs = signal("uhs", NT)
        x2t = signal("x2t", NT)
        x2h = signal("x2h", NT)
        vhs = signal("vhs", NT)
        dns = signal("dns", NT)
        Hs = signal("Hs", NT)
        HTs = signal("HTs", NT)
        w2g_s = signal("w2g_s", FT)
        xh = signal("xh", 2)
        xhb = signal("xhb", 1)
        a1_ps = signal("a1_ps", NT)
        be_a = signal("be_a", NT)
        be_b = signal("be_b", NT)
        Us = signal("Us", NT)
        a2_ps = signal("a2_ps", DT * NH)
        a2s = signal("a2s", DT * NH)
        y_ps = signal("y_ps", NT)
        ys = signal("ys", NT)
        yrelu = signal("yrelu", NT)
        cs_ps = signal("cs_ps", 1)
        css = signal("css", 1)
        shs = signal("shs", NT)
        h2T_ps = signal("h2T_ps", FT * NH)
        h2Ts = signal("h2Ts", FT * NH)
        x2_ps = signal("x2_ps", NT)
        x2s = signal("x2s", NT)
        a3_ps = signal("a3_ps", NT)
        v2s = signal("v2s", NT)
        a4_ps = signal("a4_ps", NT)
        x2f = signal("x2f", NT)
        m3_ps = signal("m3_ps", 1)
        m3s = signal("m3s", 1)
        u3s = signal("u3s", 1)
        cjs = signal("cjs", NT)
        t3_ps = signal("t3_ps", DT * NH)
        t3s = signal("t3s", DT * NH)
        v3_ps = signal("v3_ps", NT)
        v3s = signal("v3s", NT)
        s3_ps = signal("s3_ps", NH * NT)
        e3s = signal("e3s", NH * NT)
        p3s = signal("p3s", NH * NT)
        o3_ps = signal("o3_ps", NT)
        rd3 = signal("rd3", NT)
        x3s = signal("x3s", NT)

        NW = 7 + 6 + 4

        def stand(engine, waited):
            engine.sem_inc(waited.sem, 1)

        INVERT, SPREAD, COPY, WEIGH, NORMALISE, PROJECT, ADD = 4, 5, 6, 6, 9, 10, 11
        PARTS = (3, 3, 2)
        STEPS = UNITS + HEADS + 2

        def group_due(u, lag):
            g, rest = divmod(u - lag, HPG)
            return g if rest == 0 and 0 <= g < NT * GROUPS else None

        def tile_due(u, lag):
            g = group_due(u, lag)
            return g // GROUPS if g is not None and g % GROUPS == GROUPS - 1 else None

        TBANKS = 3
        turns = []
        for u in range(STEPS):
            if tile_due(u, PROJECT) is not None:
                turns.append((tile_due(u, PROJECT), "out"))
            if u < UNITS:
                turns += [(u, 0), (u, 1)]

        def turn_bank(use):
            return 4 + turns.index(use) % TBANKS

        def evacuates_both(u):
            return u % BOTH == BOTH - 1

        def by_act(u):
            return u + 1 + (u + 1) // BOTH

        def by_dve(u):
            return u + 1 - (u + 1) // BOTH

        KQ = ((0, 0, 0), (0, 0, 1), (0, 1, 0), (1, 0, 0), (1, 0, 1), (0, 1, 1), (1, 1, 0), (1, 1, 1))
        K_DONE = 5

        def last_of(n):
            return n // (GROUPS * NH), n // NH % GROUPS, n % NH

        def bank(t):
            return (4 + t) % NT

        def after(l, s):
            return NH * l + s + 1

        def rows(t):
            return slice(t * P, (t + 1) * P)

        def half(n):
            return slice(n * HALF, (n + 1) * HALF)

        def heads_of(t):
            return t[:, :].rearrange("p (a n) -> p a n", n=P)

        block = ctx.enter_context(nc.Block())

        @block.sync
        def _(sp):
            def load(dst, src):
                sp.dma_start(dst, src).then_inc(weights_in.sem, 16)

            load(wqk0s[:], wqkT0.rearrange("(t p) d -> p t d", p=P))
            load(W0[:, :, D:2 * D], wv0.rearrange("(t p) d -> p t d", p=P))
            for i in range(2):
                load(w3s[:, i], w3attn[i].rearrange("(t p) d -> p t d", p=P))
            load(Wo1[:], w1attn[3].rearrange("(t p) d -> p t d", p=P))
            load(W1h[:], w1T.rearrange("(t p) d -> p t d", p=P))
            load(W2g[:], w2T.rearrange("(t p) d -> p t d", p=P))
            for dst, src in ((bq1c, bq1), (bk1c, bk1), (bq3c, bq3), (bk3c, bk3), (gammac, gamma), (betac, beta)):
                load(dst[:], src)
            for dst, src in ((bv1B, bv1), (bo1B, bo1), (b2B, b2), (bv3B, bv3)):
                load(dst[:], src.partition_broadcast(P))

            def load_x(b):
                sp.dma_start(xn[:], x_in[bass.ds(b, 1)].rearrange("o (t p) d -> p (o t) d", p=P)).then_inc(x_in_s.sem, 16)
                sp.dma_start(mask[:], mask_in[bass.ds(b, 1)].rearrange("o p t -> p (o t)")).then_inc(x_in_s.sem, 16)

            def load_adj(b):
                sp.dma_start(adjN[:], adj_in[bass.ds(b, 1)].rearrange("o (t p) n -> p (o t) n", p=P)).then_inc(adj_in_s.sem, 16)

            def load_w1():
                for i in range(3):
                    sp.dma_start(W1[:, i], w1attn[i].rearrange("(t p) d -> p t d", p=P)).then_inc(w1_in.sem, 16)

            load_w1()
            sp.sem_inc(x_free.sem, 1)
            load_adj(0)
            sp.wait_ge(setup_dve.sem, 5)
            load_x(0)

            def batch(b, last):
                sp.wait_ge(*lo_s(b, K_DONE))
                stand(sp, waited_sp)
                for dst, parts in ((kS, (khi, khi, klo, klo)), (qS, (qhi, qlo, qhi, qlo))):
                    if dst is qS:
                        sp.wait_ge(*lo_s(b, 2 * GROUPS * NH))
                        stand(sp, waited_sp)
                    for j in range(HPG - 1):
                        done = kS_in if dst is kS else qS_in[j]
                        for r, src in enumerate(parts):
                            to = dst[HD * r:HD * r + HD].rearrange("p (g j) n -> p g j n", j=HPG)[:, :, j]
                            sp.dma_start(to.bitcast(F32), src[HD * j:HD * j + HD].bitcast(F32)).then_inc(done.sem, 16)
                sp.wait_ge(*pv_ps(b, NT * GROUPS))
                stand(sp, waited_sp)
                if not last:
                    load_w1()
                sp.dma_start(W1h[:], w1T.rearrange("(t p) d -> p t d", p=P)).then_inc(w2_in.sem, 16)
                sp.dma_start(W2g[:], w2T.rearrange("(t p) d -> p t d", p=P)).then_inc(w2_in.sem, 16)
                sp.dma_start(b1B[:], b1.partition_broadcast(P)).then_inc(w2_in.sem, 16)
                sp.dma_start(wB[:], adj_in[bass.ds(b, 1)][0, 0].partition_broadcast(P)).then_inc(wB_in.sem, 16)
                sp.wait_ge(*a3_ps(b, NT))
                stand(sp, waited_sp)
                for i, w in enumerate(w3attn):
                    sp.dma_start(W3v[:, :, 0:D] if i == 2 else W3[:, i], w.rearrange("(t p) d -> p t d", p=P)).then_inc(w3_in.sem, 16)
                if not last:
                    load_x(b + 1)
                    load_adj(b + 1)
                sp.wait_ge(*x3s(b, NT))
                stand(sp, waited_sp)
                sp.dma_start(out[bass.ds(b, 1)].rearrange("o (t p) d -> p (o t) d", p=P), x[:]).then_inc(out_s.sem, 16)
                sp.wait_ge(*out_s(b, 16))
                sp.sem_inc(x_free.sem, 1)

            with sp.Fori(0, B - 1) as b:
                batch(b, False)
            batch(B - 1, True)

        @block.gpsimd
        def _(pool):
            pool.memset(ident[:], 0.0).then_inc(consts_ready.sem, 1)
            pool.wait_ge(consts_ready.sem, 1)
            pool.affine_select(out=ident[:], in_=ident[:], compare_op=ALU.not_equal, fill=1.0, base=0,
                               pattern=[[-1, P]], channel_multiplier=1).then_inc(consts_ready.sem, 1)
            pool.memset(ones[:], 1.0).then_inc(consts_ready.sem, 1)
            pool.memset(mhalf[:], -0.5).then_inc(consts_ready.sem, 1)
            pool.wait_ge(consts_ready.sem, 4)

            def norm_scale(b, l, *halves):
                for s in halves or range(NH):
                    of = slice(TPH * s, TPH * (s + 1))
                    pool.wait_ge(*mvs(b, TPH * after(l, s)))
                    stand(pool, waited_pool)
                    pool.tensor_scalar(ve[:, of], mv[:, of, 1], EPS, 1.0, ALU.add, ALU.mult).then_inc(ves.sem, 1)
                    pool.wait_ge(*ves(b, after(l, s)))
                    pool.tensor_tensor(rstd[:, of], ve[:, of], mhalf[:, of], ALU.pow).then_inc(rstds.sem, 1)

            def batch(b, last):
                norm_scale(b, 1)
                pool.wait_ge(*hs(b, 2 * NT))
                pool.tensor_tensor(x[:], x[:], bo1B[:].unsqueeze(1).broadcast_to([P, NT, D]), ALU.add).then_inc(xbo.sem, 1)
                for g in range(NT * GROUPS):
                    pool.wait_ge(*invs(b, g + 1))
                    if g:
                        pool.wait_ge(*R_ps(b, g))
                    stand(pool, waited_pool)
                    pool.tensor_scalar(rs[:], sm[:, HPG * g:HPG * g + HPG].unsqueeze(2).broadcast_to([P, HPG, HD]),
                                       1.0, None, ALU.mult).then_inc(rss.sem, 1)
                    if g % GROUPS == GROUPS - 1:
                        t = g // GROUPS
                        pool.wait_ge(*zs(b, HEADS * (t + 1)))
                        if t == NT - 2:
                            norm_scale(b, 2, 0)
                        stand(pool, waited_pool)
                        pool.tensor_scalar(H[:, t], adjN[:, t], 0.0, 0.0, ALU.is_equal, ALU.is_equal).then_inc(Hs.sem, 1)
                norm_scale(b, 2, 1)
                pool.wait_ge(*hls(b, NT))
                stand(pool, waited_pool)
                pool.tensor_scalar(h[:, :, 0:D], h[:, :, 0:D], 0.0, None, ALU.max).then_inc(xh.sem, 1)
                pool.wait_ge(*xh(b, 1))
                pool.tensor_tensor(x[:], x[:], h[:, :, 0:D], ALU.add).then_inc(xh.sem, 1)
                pool.wait_ge(*xh(b, 2))
                pool.tensor_tensor(x[:], x[:], b2B[:].unsqueeze(1).broadcast_to([P, NT, D]), ALU.add).then_inc(xhb.sem, 1)
                norm_scale(b, 3)
                pool.wait_ge(*a4_ps(b, NT))
                stand(pool, waited_pool)
                pool.memset(v3[:, :, D:HW], 1.0).then_inc(ones_col.sem, 1)
                norm_scale(b, 4)
                if not last:
                    norm_scale(b + 1, 0)

            norm_scale(0, 0)
            with pool.Fori(0, B - 1) as b:
                batch(b, False)
            batch(B - 1, True)

        @block.vector
        def _(dve):
            dve.wait_ge(weights_in.sem, 16 * NW)
            for t in range(FT):
                dve.tensor_copy(betaB[:, t], betac[:, t:t + 1].broadcast_to([P, P])).then_inc(beta_bc.sem, 1)
            dve.tensor_tensor(bqk[:], bq3c[:], bk3c[:], ALU.mult).then_inc(setup_dve.sem, 1)
            dve.wait_ge(setup_pe.sem, 1)
            dve.tensor_copy(W0[:, 0, 0:D], ps[:, 0, 0:D]).then_inc(setup_dve.sem, 1)
            dve.tensor_copy(W0[:, 1, 0:D], ps[:, 1, 0:D]).then_inc(setup_dve.sem, 1)
            dve.wait_ge(setup_pe.sem, 2)
            dve.tensor_copy(cB[:], ps[:, 2, 0:D]).then_inc(setup_dve.sem, 1)
            dve.wait_ge(setup_pe.sem, 3)
            dve.tensor_copy(fold[:], ps[:, 3, 0:2 * DT + 1]).then_inc(setup_dve.sem, 1)
            dve.wait_ge(setup_dve.sem, 5)

            dve.wait_ge(consts_ready.sem, 4)
            for i, blocks in enumerate(((0, 1), (2, 3), (0, 2), (1, 3))):
                for r in range(P // HD):
                    dve.tensor_scalar(pick[:, i, HD * r:HD * (r + 1)], ident[:, P - HD:P], float(r in blocks), None,
                                      ALU.mult).then_inc(picks.sem, 1)

            def statistics(b, l, t, src):
                dve.bn_stats(stats[:, t], src).then_inc(stat.sem, 1)

            def aggregate(b, l, t):
                dve.wait_ge(*stat(b, NT * l + t + 1))
                stand(dve, waited_dve)
                dve.bn_aggr(mv[:, t], stats[:, t]).then_inc(mvs.sem, 1)

            def shift(b, l, s):
                of = slice(TPH * s, TPH * (s + 1))
                dve.wait_ge(*rstds(b, after(l, s)))
                dve.wait_ge(*mvs(b, TPH * after(l, s)))
                dve.scalar_tensor_tensor(nmr[:, of], mv[:, of, 0], -1.0, rstd[:, of], ALU.mult, ALU.mult).then_inc(nmrs.sem, 1)

            def norm0(b, t):
                if t == 0:
                    dve.wait_ge(*x_in_s(b, 32))
                if t < NT:
                    statistics(b, 0, t, xn[:, t])
                if 1 <= t <= NT:
                    aggregate(b, 0, t - 1)
                if t in (TPH + 2, NT + 2):
                    shift(b, 0, (t - 3) // TPH)

            def mask_h(b, t):
                dve.wait_ge(*hs(b, t + 1))
                dve.tensor_scalar(mh[:, t], h[:, t, 0:D], mask[:, t:t + 1], None, ALU.mult).then_inc(mhs.sem, 1)

            def hT_copies(b, n, s):
                for c in range(DT):
                    k = n * 2 * DT + s * DT + c
                    dve.wait_ge(*hT_ps(b, k + 1))
                    dve.tensor_copy((hT, hT1, hT)[n][:, c, half(s)], ps[:, 4 + 2 * s + c]).then_inc(hTs.sem, 1)

            def batch(b, last):
                def lower(lo, hi, t, upper_done, done):
                    dve.wait_ge(*upper_done(b, t + 1))
                    dve.scalar_tensor_tensor(lo[:, t], ps[:, bank(t), 0:D], be[:, 1, t:t + 1], hi[:, t].bitcast(F32),
                                             ALU.mult, ALU.subtract).then_inc(done.sem, 1)

                dve.tensor_scalar(mask16[:], mask[:], W_SCALE, None, ALU.mult).then_inc(chain.sem, 1)
                hT_copies(b, 0, 0)
                for n in range(1, NT * NH, 2):
                    if n == 5:
                        hT_copies(b, 0, 1)
                    dve.wait_ge(*aT_ps(b, n + 1))
                    jt, s = n // NH, n % NH
                    dve.tensor_copy(adjT[:, jt, half(s)], ps[:, n % 4]).then_inc(aT_dve.sem, 1)
                for t in range(NT):
                    dve.wait_ge(*agg_ps(b, t + 1))
                    dve.wait_ge(*gs(b, t + 1))
                    if t:
                        dve.wait_ge(*wrs(b, t))
                    dve.tensor_tensor_reduce(E3[:, 0, 0:D], ps[:, 6 + t % 2, 0:D], G[:, t], 1.0, 0.0,
                                             ALU.mult, ALU.add, sw[:, 0, t:t + 1]).then_inc(wrs.sem, 1)
                dve.wait_ge(*wrs(b, NT))
                dve.wait_ge(*chain(b, 1))
                dve.tensor_tensor(sw[:, 1], sw[:, 0], mask16[:], ALU.mult).then_inc(chain.sem, 1)
                dve.wait_ge(*chain(b, 2))
                dve.reduce_max(s1[:, 0:1], sw[:, 1], AX.X).then_inc(chain.sem, 1)
                dve.wait_ge(*chain(b, 3))
                dve.tensor_copy(E3[:, 1, 0:P], s1[:, 0:1].broadcast_to([P, P])).then_inc(wm_bc.sem, 1)
                dve.wait_ge(*wmT_ps(b, 1))
                dve.tensor_reduce(s1[:, 1:2], ps[:, 4, 0:P], AX.X, ALU.max, negate=True).then_inc(nwms.sem, 1)
                dve.wait_ge(*esum_ps(b, 1))
                dve.reciprocal(s1[:, 3:4], ps[:, 5, 0:1]).then_inc(chain.sem, 1)
                dve.wait_ge(*chain(b, 4))
                dve.tensor_scalar(sw[:, 3], sw[:, 2], s1[:, 3:4], None, ALU.mult).then_inc(chain.sem, 1)
                dve.wait_ge(*chain(b, 5))
                dve.wait_ge(*x_free(b, 1))
                def residual0(t):
                    dve.wait_ge(*V_ps(b, t // 2 * 2 + 2))
                    dve.scalar_tensor_tensor(x[:, t], ps[:, t // 2, (t % 2) * D:(t % 2 + 1) * D], sw[:, 3, t:t + 1],
                                             xn[:, t], ALU.mult, ALU.add).then_inc(x0s.sem, 1)

                def statistics1(t):
                    dve.wait_ge(*x0s(b, t + 1))
                    statistics(b, 1, t, x[:, t])

                residual0(0)
                for s in range(NH):
                    for t in range(TPH * s, TPH * (s + 1)):
                        if t + 1 < NT and t != TPH:
                            residual0(t + 1)
                        statistics1(t)
                        if t % TPH:
                            aggregate(b, 1, t - 1)
                    aggregate(b, 1, TPH * (s + 1) - 1)
                    if s == 0:
                        residual0(TPH + 1)
                        shift(b, 1, 0)
                hT_copies(b, 1, 0)
                shift(b, 1, 1)
                def add_bv(s):
                    for t in range(TPH * s, TPH * (s + 1)):
                        dve.wait_ge(*v_ps(b, t + 1))
                        dve.tensor_tensor(v[:, t], ps[:, 4 + t % 4, 0:D], bv1B[:], ALU.add).then_inc(vs.sem, 1)

                for n in range(2 * GROUPS * NH):
                    s, w, g = KQ[n]
                    bias, hi, lo = ((bk1c, khi, klo), (bq1c, qhi, qlo))[w]
                    if n == GROUPS:
                        hT_copies(b, 1, 1)
                    dve.wait_ge(*hi_s(b, n + 1))
                    dve.scalar_tensor_tensor(lo[:, g, half(s)], ps[:, n % 4], bias[:, g:g + 1],
                                             hi[:, g, half(s)].bitcast(F32), ALU.add, ALU.subtract).then_inc(lo_s.sem, 1)
                add_bv(0)
                add_bv(1)

                def evacuate(u):
                    if evacuates_both(u):
                        return
                    bank = turn_bank((u, 1))
                    dve.wait_ge(*T_ps(b, 2 * u + 2))
                    if u >= PTS:
                        dve.wait_ge(*pv_ps(b, (u - PTS) // HPG + 1))
                    dve.tensor_copy(PT[:, u % PTS, NT // 2:NT], heads_of(ps[:, bank])).then_inc(PT_dve.sem, 1)

                def inverse_sums(g):
                    dve.wait_ge(*exps(b, HPG * (g + 1)))
                    dve.reciprocal(sm[:, HPG * g:HPG * g + HPG], sm[:, HPG * g:HPG * g + HPG]).then_inc(invs.sem, 1)

                def normalise(g):
                    dve.wait_ge(*pv_ps(b, g + 1))
                    if g >= GROUPS:
                        dve.wait_ge(*o_ps(b, (g - GROUPS) // GROUPS + 1))
                    dve.tensor_tensor(ctxn[:, g % GROUPS], ps[:, 7, 0:P], Rs[:], ALU.mult).then_inc(ctxs.sem, 1)

                def add_output(t):
                    dve.wait_ge(*o_ps(b, t + 1))
                    if t == 0:
                        dve.wait_ge(*xbo(b, 1))
                    dve.tensor_tensor(x[:, t], ps[:, turn_bank((t, "out")), 0:D], x[:, t], ALU.add).then_inc(x1s.sem, 1)

                def split_h(s):
                    shift(b, 2, s)
                    dve.wait_ge(*nmrs(b, after(2, s)))
                    for t in range(TPH * s, TPH * (s + 1) + 1):
                        if t < TPH * (s + 1):
                            dve.tensor_scalar(h[:, t, 0:D], x[:, t], rstd[:, t:t + 1], nmr[:, t:t + 1], ALU.mult, ALU.add).then_inc(h_d.sem, 1)
                        if t > TPH * s:
                            dve.wait_ge(*h_d(b, t))
                            dve.wait_ge(*hhs(b, t))
                            dve.scalar_tensor_tensor(hl[:, t - 1], h[:, t - 1, 0:D], 0.0, hh[:, t - 1, 0:D].bitcast(F32),
                                                     ALU.max, ALU.subtract).then_inc(hls.sem, 1)

                for u in range(STEPS):
                    if u == UNITS + 3:
                        split_h(0)
                    if u < UNITS:
                        dve.wait_ge(*S_ps(b, u + 1))
                        if u >= ZS:
                            dve.wait_ge(*T_ps(b, 2 * (u - ZS) + 2))
                        stand(dve, waited_dve)
                        dve.tensor_tensor_reduce(Z[:, u % ZS], ps[:, 2 * (u % 2):2 * (u % 2) + 2].rearrange("p a n -> p (a n)"),
                                                 adjN[:, u // HEADS], SCORE_SCALE, LOWEST, ALU.mult, ALU.max,
                                                 nm[:, u:u + 1]).then_inc(zs.sem, 1)
                    if u < UNITS:
                        dve.wait_ge(*zs(b, u + 1))
                        dve.tensor_scalar(nm[:, u:u + 1], nm[:, u:u + 1], -1.0, None, ALU.mult).then_inc(nms.sem, 1)
                    if (g := group_due(u, NORMALISE)) is not None:
                        normalise(g)
                    if (t := tile_due(u, ADD)) is not None:
                        add_output(t)
                    if (t := tile_due(u, ADD + 1)) is not None:
                        dve.wait_ge(*x1s(b, t + 1))
                        statistics(b, 2, t, x[:, t])
                    if (t := tile_due(u, ADD + 2)) is not None:
                        aggregate(b, 2, t)
                    if 2 <= u < UNITS + 2:
                        evacuate(u - 2)
                    if (g := group_due(u, INVERT)) is not None:
                        inverse_sums(g)

                split_h(1)
                for t in range(NT):
                    dve.tensor_scalar(HT[:, t], adjT[:, t], 0.0, None, ALU.not_equal).then_inc(HTs.sem, 1)
                for t in range(NT + 1):
                    if t < NT:
                        dve.wait_ge(*a1_ps(b, t + 1))
                        dve.tensor_scalar(be[:, 0, t:t + 1], ps[:, bank(t), D:D + 1], 1.0, None, ALU.max).then_inc(be_a.sem, 1)
                        dve.wait_ge(*be_a(b, t + 1))
                        dve.reciprocal(be[:, 1, t:t + 1], be[:, 0, t:t + 1]).then_inc(be_b.sem, 1)
                    if t:
                        lower(Ul, Uh, t - 1, uhs, Us)
                dve.wait_ge(*wB_in(b, 16))
                for t in range(NT):
                    dve.wait_ge(*Hs(b, t + 1))
                    if t:
                        dve.wait_ge(*dns(b, t))
                    dve.scalar_tensor_tensor(junk[:], H[:, t].bitcast(F32), 1.0, wB[:], ALU.mult, ALU.mult,
                                             accum_out=dn[:, 0, t:t + 1]).then_inc(dns.sem, 1)
                dve.wait_ge(*dns(b, NT))
                dve.tensor_scalar(dn[:, 1], dn[:, 0], 0.0, None, ALU.is_gt).then_inc(chain.sem, 1)
                dve.tensor_scalar(dn[:, 2], dn[:, 0], TINY, None, ALU.max).then_inc(chain.sem, 1)
                dve.wait_ge(*chain(b, 7))
                dve.reciprocal(dn[:, 3], dn[:, 2]).then_inc(chain.sem, 1)
                dve.wait_ge(*chain(b, 8))
                dve.tensor_tensor(dn[:, 3], dn[:, 3], dn[:, 1], ALU.mult).then_inc(chain.sem, 1)
                dve.wait_ge(*w2_in(b, 48))
                for t in range(FT):
                    dve.tensor_scalar(W2g[:, t], W2g[:, t], gammac[:, t:t + 1], None, ALU.mult).then_inc(w2g_s.sem, 1)
                dve.wait_ge(*chain(b, 9))
                def copy_h2T(s):
                    for f in range(FT):
                        n = FT * s + f
                        dve.wait_ge(*h2T_ps(b, n + 1))
                        dve.tensor_copy(h2T[:, f, half(s)], ps[:, 4 + n % 4]).then_inc(h2Ts.sem, 1)

                for t in range(NT + 1):
                    if t == NT - 1:
                        copy_h2T(0)
                    if t < NT:
                        dve.wait_ge(*y_ps(b, t + 1))
                        dve.scalar_tensor_tensor(h2[:, t], ps[:, t % 4], dn[:, 3, t:t + 1], b1B[:], ALU.mult,
                                                 ALU.add).then_inc(ys.sem, 1)
                    if t:
                        dve.wait_ge(*yrelu(b, t))
                        statistics(b, 3, t - 1, h2[:, t - 1])
                        aggregate(b, 3, t - 1)
                    if t == TPH + 1:
                        shift(b, 3, 0)
                dve.wait_ge(*cs_ps(b, 1))
                dve.tensor_copy(cs[:], ps[:, 0, 0:D]).then_inc(css.sem, 1)
                dve.wait_ge(*css(b, 1))
                shift(b, 3, 1)
                dve.wait_ge(*nmrs(b, after(3, 1)))
                dve.wait_ge(*xh(b, 2))
                for t in range(NT):
                    if t == TPH - 1:
                        copy_h2T(1)
                    if t >= 2:
                        dve.wait_ge(*x2t(b, t - 1))
                    dve.scalar_tensor_tensor(shiftB[:, t % 2], cs[:], nmr[:, t:t + 1], cB[:], ALU.mult, ALU.add).then_inc(shs.sem, 1)
                    dve.wait_ge(*x2_ps(b, t + 1))
                    dve.wait_ge(*shs(b, t + 1))
                    dve.scalar_tensor_tensor(h[:, t, 0:D], ps[:, t % 4, 0:D], rstd[:, t:t + 1], shiftB[:, t % 2],
                                             ALU.mult, ALU.add).then_inc(x2t.sem, 1)
                    dve.wait_ge(*x2h(b, t + 1))
                    dve.tensor_tensor(Ul[:, t], h[:, t, 0:D], Uh[:, t].bitcast(F32), ALU.subtract).then_inc(x2s.sem, 1)
                for t in range(NT):
                    dve.wait_ge(*a3_ps(b, t + 1))
                    lower(Vl, Vh, t, vhs, v2s)
                dve.tensor_copy(W3v[:, :, D], fold[:, DT:2 * DT]).then_inc(u3s.sem, 1)
                dve.wait_ge(*xhb(b, 1))
                for t in range(NT + 2):
                    if t < NT:
                        dve.wait_ge(*a4_ps(b, t + 1))
                        dve.scalar_tensor_tensor(x[:, t], ps[:, bank(t), 0:D], dn[:, 3, t:t + 1], x[:, t], ALU.mult,
                                                 ALU.add).then_inc(x2f.sem, 1)
                    if 1 <= t <= NT:
                        dve.wait_ge(*x2f(b, t))
                        statistics(b, 4, t - 1, x[:, t - 1])
                    if t >= 2:
                        aggregate(b, 4, t - 2)
                    if t == TPH + 3:
                        shift(b, 4, 0)
                shift(b, 4, 1)
                hT_copies(b, 2, 0)
                hT_copies(b, 2, 1)
                for t in range(NT):
                    dve.wait_ge(*v3_ps(b, t + 1))
                    if t == 0:
                        dve.wait_ge(*ones_col(b, 1))
                    dve.tensor_scalar(cj[:, t:t + 1], ps[:, 4 + t % 4, D:D + 1], fold[:, 2 * DT:2 * DT + 1], None,
                                      ALU.add).then_inc(cjs.sem, 1)
                    dve.tensor_tensor(v3[:, t, 0:D], ps[:, 4 + t % 4, 0:D], bv3B[:], ALU.add).then_inc(v3s.sem, 1)

                def mask_exp(n):
                    s, kt = n // NT, n % NT
                    dve.wait_ge(*e3s(b, n + 1))
                    dve.tensor_tensor(P3[:, s, kt], E3[:, n % 2], adjT[:, kt, half(s)], ALU.mult).then_inc(p3s.sem, 1)

                def finish(t):
                    dve.wait_ge(*o3_ps(b, t + 1))
                    dve.reciprocal(rden[:, t:t + 1], ps[:, 6 + t % 2, D:D + 1]).then_inc(rd3.sem, 1)
                    dve.wait_ge(*rd3(b, t + 1))
                    dve.scalar_tensor_tensor(x[:, t], ps[:, 6 + t % 2, 0:D], rden[:, t:t + 1], x[:, t], ALU.mult,
                                             ALU.add).then_inc(x3s.sem, 1)

                for n in range(NH * NT):
                    mask_exp(n)
                    if not last and n >= 4:
                        norm0(b + 1, n - 4)
                for t in range(NT):
                    finish(t)
                    if not last:
                        mask_h(b + 1, t)

            for t in range(NT + 3):
                norm0(0, t)
            for t in range(NT):
                mask_h(0, t)
            with dve.Fori(0, B - 1) as b:
                batch(b, False)
            batch(B - 1, True)

        @block.scalar
        def _(act):
            def normalise(b, l, k, src):
                for t in range(NT):
                    if t % TPH == 0:
                        act.wait_ge(*nmrs(b, after(l, t // TPH)))
                    act.activation(h[:, t, 0:D], src[:, t], ACT.Relu, bias=nmr[:, t:t + 1],
                                   scale=rstd[:, t:t + 1]).then_inc(hs.sem, 1)

            def batch(b, last):
                for n in range(0, NT * NH, 2):
                    act.wait_ge(*aT_ps(b, n + 1))
                    jt, s = n // NH, n % NH
                    act.activation(adjT[:, jt, half(s)], ps[:, n % 4], ACT.Copy).then_inc(aT_act.sem, 1)
                for t in range(NT):
                    act.wait_ge(*g_ps(b, t + 1))
                    act.activation(G[:, t], ps[:, 4 + t % 2, 0:D], ACT.Copy).then_inc(gs.sem, 1)
                act.wait_ge(*nwms(b, 1))
                act.activation(sw[:, 2], sw[:, 1], ACT.Exp, bias=s1[:, 1:2], accum_out=s1[:, 2:3]).then_inc(es.sem, 1)
                normalise(b, 1, 1, x)
                for n in range(2 * GROUPS * NH):
                    s, w, g = KQ[n]
                    bias, hi = ((bk1c, khi), (bq1c, qhi))[w]
                    act.wait_ge(*kq_ps(b, n + 1))
                    act.activation(hi[:, g, half(s)], ps[:, n % 4], ACT.Identity, bias=bias[:, g:g + 1]).then_inc(hi_s.sem, 1)

                for n in range(2 * GROUPS * NH):
                    w, g, s = last_of(n)
                    act.wait_ge(*last_ps(b, n + 1))
                    act.activation((kS, qS)[w][:, HPG * g + HPG - 1, half(s)], ps[:, n % 4], ACT.Copy).then_inc(lasts.sem, 1)

                def evacuate(u):
                    for half_of_u in range(1 + evacuates_both(u)):
                        bank = turn_bank((u, half_of_u))
                        act.wait_ge(*T_ps(b, 2 * u + half_of_u + 1))
                        if u >= PTS:
                            act.wait_ge(*pv_ps(b, (u - PTS) // HPG + 1))
                        first = NT // 2 * half_of_u
                        act.activation(PT[:, u % PTS, first:first + NT // 2], heads_of(ps[:, bank]), ACT.Copy).then_inc(PT_act.sem, 1)

                for u in range(STEPS):
                    if (g := group_due(u, COPY)) is not None:
                        act.wait_ge(*R_ps(b, g + 1))
                        act.activation(Rs[:], ps[:, 7, P:2 * P], ACT.Copy).then_inc(Rss.sem, 1)
                    if u < UNITS:
                        act.wait_ge(*nms(b, u + 1))
                        act.activation(Z[:, u % ZS], Z[:, u % ZS], ACT.Exp, bias=nm[:, u:u + 1],
                                       accum_out=sm[:, u:u + 1]).then_inc(exps.sem, 1)
                    if 1 <= u < UNITS + 1:
                        evacuate(u - 1)
                act.wait_ge(*pv_ps(b, NT * GROUPS - 1))
                act.activation(hh[:, :, D:HW], ones[:, 0:2 * NT].rearrange("p (t c) -> p t c", c=2), ACT.Copy).then_inc(ones_h.sem, 1)
                for t in range(NT):
                    if t % TPH == 0:
                        act.wait_ge(*nmrs(b, after(2, t // TPH)))
                    act.activation(hh[:, t, 0:D], x[:, t], ACT.Relu, bias=nmr[:, t:t + 1], scale=rstd[:, t:t + 1]).then_inc(hhs.sem, 1)
                for t in range(NT):
                    act.wait_ge(*be_b(b, t + 1))
                    act.activation(Uh[:, t], ps[:, bank(t), 0:D], ACT.Copy, scale=be[:, 1, t:t + 1]).then_inc(uhs.sem, 1)
                for n in range(DT * NH):
                    act.wait_ge(*a2_ps(b, n + 1))
                    act.activation(A2T[:, n % DT, half(n // DT)], ps[:, 4 + n], ACT.Copy).then_inc(a2s.sem, 1)

                for t in range(NT):
                    act.wait_ge(*ys(b, t + 1))
                    act.activation(h2[:, t], h2[:, t], ACT.Relu).then_inc(yrelu.sem, 1)
                for t in range(NT):
                    act.wait_ge(*x2t(b, t + 1))
                    act.activation(Uh[:, t], h[:, t, 0:D], ACT.Copy).then_inc(x2h.sem, 1)
                for t in range(NT):
                    act.wait_ge(*a3_ps(b, t + 1))
                    act.activation(Vh[:, t], ps[:, bank(t), 0:D], ACT.Copy, scale=be[:, 1, t:t + 1]).then_inc(vhs.sem, 1)
                act.wait_ge(*m3_ps(b, 1))
                act.activation(M3[:].rearrange("p c d -> p (c d)"), ps[:, bank(0)], ACT.Copy).then_inc(m3s.sem, 1)
                normalise(b, 4, 2, x)
                for n in range(DT * NH):
                    s, f = n // DT, n % DT
                    act.wait_ge(*t3_ps(b, n + 1))
                    act.activation(t3T[:, f, half(s)], ps[:, n % 4], ACT.Identity, bias=fold[:, f:f + 1]).then_inc(t3s.sem, 1)
                for n in range(NH * NT):
                    act.wait_ge(*s3_ps(b, n + 1))
                    if n >= 2:
                        act.wait_ge(*p3s(b, n - 1))
                    act.wait_ge(*cjs(b, n % NT + 1))
                    act.activation(E3[:, n % 2], ps[:, n % 4], ACT.Exp, bias=cj[:, n % NT:n % NT + 1]).then_inc(e3s.sem, 1)

                if not last:
                    normalise(b + 1, 0, 0, xn)

            act.wait_ge(setup_dve.sem, 5)
            normalise(0, 0, 0, xn)
            with act.Fori(0, B - 1) as b:
                batch(b, False)
            batch(B - 1, True)

        @block.tensor
        def _(pe):
            def product(dst, pairs):
                for i, (lhsT, rhs) in enumerate(pairs):
                    mm = pe.matmul(dst, lhsT, rhs, start=(i == 0), stop=(i == len(pairs) - 1))
                return mm

            pe.wait_ge(weights_in.sem, 16 * NW)
            for a in range(DT):
                mm = product(ps[:, a, 0:D], [(wqk0s[:, c, rows(a)], wqk0s[:, DT + c]) for c in range(DT)])
            mm.then_inc(setup_pe.sem, 1)
            pe.wait_ge(consts_ready.sem, 4)
            pe.wait_ge(beta_bc.sem, FT)
            product(ps[:, 2, 0:D], [(betaB[:, t], W2g[:, t]) for t in range(FT)]).then_inc(setup_pe.sem, 1)
            for a in range(DT):
                product(ps[:, 3, a:a + 1], [(w3s[:, 0, c, rows(a)], bk3c[:, c:c + 1]) for c in range(DT)])
            for a in range(DT):
                product(ps[:, 3, DT + a:DT + a + 1], [(w3s[:, 1, c, rows(a)], bq3c[:, c:c + 1]) for c in range(DT)])
            pe.wait_ge(setup_dve.sem, 1)
            product(ps[:, 3, 2 * DT:2 * DT + 1], [(ones[:], bqk[:, c:c + 1]) for c in range(DT)]).then_inc(setup_pe.sem, 1)
            pe.wait_ge(setup_dve.sem, 5)

            def keep_warm(bank, count):
                for _ in range(count):
                    pe.matmul(ps[:, bank], ident[:], adjT[:, 0, half(0)], start=True, stop=True)

            def transpose_h(b, k, s):
                for c in range(DT):
                    for a in range(TPH):
                        t = TPH * s + a
                        pe.wait_ge(*hs(b, NT * k + t + 1))
                        mm = pe.transpose(ps[:, 4 + 2 * s + c, rows(a)], h[:, t, rows(c)], ident[:])
                    mm.then_inc(hT_ps.sem, 1)

            def batch(b):
                transpose_h(b, 0, 0)
                pe.wait_ge(*adj_in_s(b, 16))
                for n in range(NT * NH):
                    jt, s = n // NH, n % NH
                    if n == 4:
                        pe.wait_ge(*hTs(b, DT))
                        transpose_h(b, 0, 1)
                    if n >= 4:
                        done = aT_act if n % 2 == 0 else aT_dve
                        pe.wait_ge(*done(b, (n - 4) // 2 + 1))
                    for a in range(TPH):
                        mm = pe.transpose(ps[:, n % 4, rows(a)], adjN[:, TPH * s + a, rows(jt)], ident[:])
                    mm.then_inc(aT_ps.sem, 1)
                pe.wait_ge(*hTs(b, 2 * DT))
                for t in range(NT):
                    if t >= 2:
                        pe.wait_ge(*gs(b, t - 1))
                    product(ps[:, 4 + t % 2, 0:D], [(hT[:, c, rows(t)], W0[:, c, 0:D]) for c in range(DT)]).then_inc(g_ps.sem, 1)
                pe.wait_ge(*mhs(b, NT))
                pe.wait_ge(*aT_act(b, NT * NH // 2))
                pe.wait_ge(*aT_dve(b, NT * NH // 2))
                for t in range(NT):
                    if t >= 2:
                        pe.wait_ge(*wrs(b, t - 1))
                    product(ps[:, 6 + t % 2, 0:D], [(adjT[:, j, rows(t)], mh[:, j]) for j in range(NT)]).then_inc(agg_ps.sem, 1)
                def values(t):
                    product(ps[:, t // 2, (t % 2) * D:(t % 2 + 1) * D],
                            [(hT[:, c, rows(t)], W0[:, c, D:2 * D]) for c in range(DT)]).then_inc(V_ps.sem, 1)

                values(0)
                pe.wait_ge(*wm_bc(b, 1))
                pe.wait_ge(*gs(b, NT))
                pe.transpose(ps[:, 4, 0:P], E3[:, 1, 0:P], ident[:]).then_inc(wmT_ps.sem, 1)
                values(1)
                pe.wait_ge(*es(b, 1))
                pe.matmul(ps[:, 5, 0:1], ones[:], s1[:, 2:3], start=True, stop=True).then_inc(esum_ps.sem, 1)
                for t in range(2, NT):
                    values(t)
                keep_warm(6, 3)
                def project_v(s):
                    for t in range(TPH * s, TPH * (s + 1)):
                        if t >= 4:
                            pe.wait_ge(*vs(b, t - 3))
                        product(ps[:, 4 + t % 4, 0:D], [(hT1[:, c, rows(t)], Wv1[:, c]) for c in range(DT)]).then_inc(v_ps.sem, 1)

                transpose_h(b, 1, 0)
                keep_warm(6, 1)
                pe.wait_ge(*hTs(b, 3 * DT))
                pe.wait_ge(*x0s(b, NT))
                pe.wait_ge(*w1_in(b, 48))
                for n in range(2 * GROUPS * NH):
                    s, w, g = KQ[n]
                    if n == GROUPS:
                        transpose_h(b, 1, 1)
                    if s == 1:
                        pe.wait_ge(*hTs(b, 4 * DT))
                    if n >= 4:
                        pe.wait_ge(*lo_s(b, n - 3))
                    product(ps[:, n % 4], [((Wk1, Wq1)[w][:, c, rows(g)], hT1[:, c, half(s)]) for c in range(DT)]).then_inc(kq_ps.sem, 1)
                project_v(0)
                pe.wait_ge(picks.sem, 16)
                for n in range(2 * GROUPS * NH):
                    w, g, s = last_of(n)
                    pe.wait_ge(*lo_s(b, 2 * GROUPS * NH))
                    if n >= 4:
                        pe.wait_ge(*lasts(b, n - 3))
                    if n == GROUPS * NH:
                        project_v(1)
                    hi, lo = ((khi, klo), (qhi, qlo))[w]
                    product(ps[:, n % 4], [(pick[:, 2 * w], hi[:, g, half(s)]), (pick[:, 2 * w + 1], lo[:, g, half(s)])]).then_inc(last_ps.sem, 1)

                def scores(u):
                    t, hd = u // HEADS, u % HEADS
                    if u >= 2:
                        pe.wait_ge(*zs(b, u - 1))
                    if u < HPG - 1:
                        pe.wait_ge(*qS_in[u](b, 64))
                    for s in range(NH):
                        mm = pe.matmul(ps[:, 2 * (u % 2) + s], qS[:, hd, rows(t)], kS[:, hd, half(s)], start=True, stop=True)
                    mm.then_inc(S_ps.sem, 1)

                def wait_bank(use):
                    if turns.index(use) < TBANKS:
                        return
                    n, what = turns[turns.index(use) - TBANKS]
                    if what == "out":
                        pe.wait_ge(*x1s(b, n + 1))
                    elif what == 0 or evacuates_both(n):
                        pe.wait_ge(*PT_act(b, by_act(n) - (what == 0 and evacuates_both(n))))
                    else:
                        pe.wait_ge(*PT_dve(b, by_dve(n)))

                def transposes(u):
                    pe.wait_ge(*exps(b, u + 1))
                    for s in range(2):
                        wait_bank((u, s))
                        for a in range(NT // 2):
                            mm = pe.transpose(ps[:, turn_bank((u, s)), rows(a)], Z[:, u % ZS, rows(NT // 2 * s + a)], ident[:])
                        mm.then_inc(T_ps.sem, 1)

                def spread_inverses(g):
                    pe.wait_ge(*rss(b, g + 1))
                    if g:
                        pe.wait_ge(*ctxs(b, g))
                    pe.matmul(ps[:, 7, P:2 * P], rs[:].rearrange("p h d -> p (h d)"),
                              ident[:], start=True, stop=True).then_inc(R_ps.sem, 1)

                def weighted_values(g, part):
                    if part == 0:
                        pe.wait_ge(*PT_act(b, by_act(HPG * g + HPG - 1)))
                        pe.wait_ge(*PT_dve(b, by_dve(HPG * g + HPG - 1)))
                        pe.wait_ge(*Rss(b, g + 1))
                    for kt in range(sum(PARTS[:part]), sum(PARTS[:part + 1])):
                        for j in range(HPG):
                            hd = HPG * (g % GROUPS) + j
                            mm = pe.matmul(ps[HD * j:HD * j + HD, 7, 0:P],
                                           v[:, kt, HD * hd:HD * hd + HD], PT[:, (HPG * g + j) % PTS, kt],
                                           start=(kt == 0), stop=(kt == NT - 1))
                    if part == len(PARTS) - 1:
                        mm.then_inc(pv_ps.sem, 1)

                def project(t):
                    pe.wait_ge(*ctxs(b, GROUPS * (t + 1)))
                    wait_bank((t, "out"))
                    product(ps[:, turn_bank((t, "out")), 0:D], [(ctxn[:, g], Wo1[:, g]) for g in range(GROUPS)]).then_inc(o_ps.sem, 1)

                pe.wait_ge(*lo_s(b, 2 * GROUPS * NH))
                pe.wait_ge(*lasts(b, 2 * GROUPS * NH - 3))
                keep_warm(0, 1)
                pe.wait_ge(*kS_in(b, 64 * (HPG - 1)))
                pe.wait_ge(*vs(b, NT))
                pe.wait_ge(*lasts(b, 2 * GROUPS * NH))
                scores(0)
                keep_warm(turn_bank((0, 1)), 1)
                scores(1)
                keep_warm(turn_bank((0, 1)), 1)
                for u in range(STEPS):
                    if (t := tile_due(u, PROJECT)) is not None:
                        project(t)
                    if u == 0:
                        transposes(u)
                    if u + 2 < UNITS:
                        scores(u + 2)
                    for part in range(len(PARTS)):
                        if (g := group_due(u, WEIGH + part)) is not None:
                            weighted_values(g, part)
                    if 0 < u < UNITS:
                        transposes(u)
                    if (g := group_due(u, SPREAD)) is not None:
                        spread_inverses(g)
                def sum_up(dst, lhs, rhs, ready, bank_free, done, tail=2):
                    def step(n, j):
                        for i in ((0, 1) if j == 0 else (1, 0)):
                            mm = pe.matmul(dst(n, i), lhs(n, j, i), rhs(n, j, i), start=(j == 0 and i == 0),
                                           stop=(j == NT - 1 and i == 0))
                        return mm
                    count = len(bank_free)
                    for j in range(NT - tail):
                        for wait in ready:
                            pe.wait_ge(*wait(b, j + 1))
                        for n in range(count):
                            if j == 0 and bank_free[n] is not None:
                                pe.wait_ge(*bank_free[n])
                            step(n, j)
                    for n in range(count):
                        for j in range(NT - tail, NT):
                            if n == 0:
                                for wait in ready:
                                    pe.wait_ge(*wait(b, j + 1))
                            mm = step(n, j)
                        mm.then_inc(done.sem, 1)

                def of_edges(hi, lo, width):
                    return (lambda t, i: ps[:, bank(t), 0:(D, width)[i == 0]], lambda t, j, i: H[:, j, rows(t)],
                            lambda t, j, i: (hi, lo)[i][:, j])

                def of_nodes(hi, lo):
                    return (lambda t, i: ps[:, bank(t), 0:D], lambda t, j, i: HT[:, j, rows(t)],
                            lambda t, j, i: (hi, lo)[i][:, j])

                pe.wait_ge(*ones_h(b, 1))
                pe.wait_ge(*PT_act(b, by_act(UNITS - 1)))
                pe.wait_ge(*PT_dve(b, by_dve(UNITS - 1)))
                sum_up(*of_edges(hh, hl, HW), (Hs, hhs, hls),
                       [{7: ctxs(b, NT * GROUPS), turn_bank((NT - 1, "out")): x1s(b, NT)}.get(bank(t)) for t in range(NT)], a1_ps)
                sum_up(lambda n, i: ps[:, 4 + n], lambda n, j, i: (Uh, Ul)[i][:, j, rows(n % DT)],
                       lambda n, j, i: HT[:, j, half(n // DT)], (HTs, Us), [Us(b, n + 1) for n in range(DT * NH)], a2_ps)
                pe.wait_ge(*w2_in(b, 48))

                def transpose_h2(s):
                    for f in range(FT):
                        n = FT * s + f
                        if n >= 4:
                            pe.wait_ge(*h2Ts(b, n - 3))
                        for a in range(TPH):
                            if f == 0:
                                pe.wait_ge(*yrelu(b, TPH * s + a + 1))
                            mm = pe.transpose(ps[:, 4 + n % 4, rows(a)], h2[:, TPH * s + a, rows(f)], ident[:])
                        mm.then_inc(h2T_ps.sem, 1)

                for t in range(NT):
                    if t == NT - 1:
                        transpose_h2(0)
                    if t % TPH == 0:
                        pe.wait_ge(*a2s(b, DT * (t // TPH + 1)))
                    if t >= 4:
                        pe.wait_ge(*ys(b, t - 3))
                    product(ps[:, t % 4], [(A2T[:, c, rows(t)], W1h[:, c]) for c in range(DT)]).then_inc(y_ps.sem, 1)
                pe.wait_ge(*a2s(b, DT * NH))
                pe.wait_ge(*w2g_s(b, FT))
                pe.wait_ge(*ys(b, TPH + 1))
                product(ps[:, 0, 0:D], [(ones[:], W2g[:, f]) for f in range(FT)]).then_inc(cs_ps.sem, 1)
                for t in range(NT):
                    if t == TPH - 1:
                        transpose_h2(1)
                    if t % TPH == 0:
                        pe.wait_ge(*h2Ts(b, FT * (t // TPH + 1)))
                    if t == 0:
                        pe.wait_ge(*css(b, 1))
                    if t < TPH:
                        pe.wait_ge(*ys(b, TPH + t + 1))
                    else:
                        pe.wait_ge(*x2t(b, t - 3))
                    product(ps[:, t % 4, 0:D], [(h2T[:, f, rows(t)], W2g[:, f]) for f in range(FT)]).then_inc(x2_ps.sem, 1)
                sum_up(*of_edges(Uh, Ul, D), (x2s,), [None] * 4 + [x2t(b, t + 1) for t in range(4, NT)], a3_ps)
                sum_up(*of_nodes(Vh, Vl), (v2s,), [v2s(b, t + 1) for t in range(NT)], a4_ps, tail=4)
                pe.wait_ge(*x2f(b, 2))
                pe.wait_ge(*w3_in(b, 48))
                for c in range(DT):
                    mm = product(ps[:, bank(0), D * c:D * (c + 1)], [(W3[:, 1, o, rows(c)], W3[:, 0, o]) for o in range(DT)])
                mm.then_inc(m3_ps.sem, 1)
                keep_warm(bank(1), 2)
                pe.wait_ge(*m3s(b, 1))
                transpose_h(b, 2, 0)
                pe.wait_ge(*x2f(b, NT))
                for n in range(DT * NH):
                    s, f = n // DT, n % DT
                    if n == DT - 1:
                        transpose_h(b, 2, 1)
                    pe.wait_ge(*hTs(b, 4 * DT + DT * (s + 1)))
                    product(ps[:, n % 4], [(M3[:, c, rows(f)], hT[:, c, half(s)]) for c in range(DT)]).then_inc(t3_ps.sem, 1)
                pe.wait_ge(*u3s(b, 1))
                for t in range(NT):
                    if t >= 4:
                        pe.wait_ge(*v3s(b, t - 3))
                    product(ps[:, 4 + t % 4, 0:D + 1], [(hT[:, c, rows(t)], W3v[:, c, 0:D + 1]) for c in range(DT)]).then_inc(v3_ps.sem, 1)
                pe.wait_ge(*t3s(b, DT * NH))
                for n in range(NH * NT):
                    s, kt = n // NT, n % NT
                    if n >= 4:
                        pe.wait_ge(*e3s(b, n - 3))
                    product(ps[:, n % 4], [(t3T[:, c, rows(kt)], hT[:, c, half(s)]) for c in range(DT)]).then_inc(s3_ps.sem, 1)
                pe.wait_ge(*v3s(b, NT))
                for t in range(NT):
                    s, a = t // TPH, t % TPH
                    pe.wait_ge(*p3s(b, NT * (s + 1)))
                    if t >= 2:
                        pe.wait_ge(*x3s(b, t - 1))
                    product(ps[:, 6 + t % 2, 0:D + 1], [(P3[:, s, j, rows(a)], v3[:, j, 0:D + 1]) for j in range(NT)]).then_inc(o3_ps.sem, 1)

            with pe.Fori(0, B) as b:
                batch(b)


def kernel(x, adj, nodemask, L0_gnn_Wqk, L0_gnn_Wv, L1_gnn_Wq, L1_gnn_bq, L1_gnn_Wk, L1_gnn_bk, L1_gnn_Wv,
           L1_gnn_bv, L1_gnn_Wo, L1_gnn_bo, L2_gnn_W1, L2_gnn_b1, L2_gnn_gamma, L2_gnn_beta, L2_gnn_W2, L2_gnn_b2,
           L3_gnn_Wq_w, L3_gnn_Wq_b, L3_gnn_Wk_w, L3_gnn_Wk_b, L3_gnn_Wv_w, L3_gnn_Wv_b):
    import numpy as np
    import concourse.bacc as bacc
    from concourse.bass_utils import run_bass_kernel_spmd

    def T(a):
        return np.ascontiguousarray(np.asarray(a).T)

    def columns(a):
        a = np.asarray(a)
        return np.swapaxes(a.reshape(*a.shape[:-1], -1, P), -1, -2)

    arrays = {
        "x_in": x, "adj_in": adj, "mask_in": columns(nodemask), "wqkT0": T(L0_gnn_Wqk), "wv0": L0_gnn_Wv,
        "wq1": T(L1_gnn_Wq), "wk1": T(L1_gnn_Wk), "wv1": T(L1_gnn_Wv), "wo1": T(L1_gnn_Wo),
        "bq1": columns(L1_gnn_bq), "bk1": columns(L1_gnn_bk), "bv1": L1_gnn_bv, "bo1": L1_gnn_bo,
        "w1T": T(L2_gnn_W1), "b1": L2_gnn_b1, "gamma": columns(L2_gnn_gamma), "beta": columns(L2_gnn_beta),
        "w2T": T(L2_gnn_W2), "b2": L2_gnn_b2,
        "wq3": L3_gnn_Wq_w, "wk3": L3_gnn_Wk_w, "wv3": T(L3_gnn_Wv_w),
        "bq3": columns(L3_gnn_Wq_b), "bk3": columns(L3_gnn_Wk_b), "bv3": L3_gnn_Wv_b,
    }
    arrays = {n: np.ascontiguousarray(a) for n, a in arrays.items()}
    nc = bacc.Bacc("TRN2", target_bir_lowering=False, num_devices=1)
    t = {n: nc.dram_tensor(n, a.shape, mybir.dt.from_np(a.dtype), kind="ExternalInput").ap() for n, a in arrays.items()}
    out = nc.dram_tensor("out", arrays["x_in"].shape, F32, kind="ExternalOutput").ap()
    build_program(nc, t["x_in"], t["adj_in"], t["mask_in"], t["wqkT0"], t["wv0"],
                  [t["wq1"], t["wk1"], t["wv1"], t["wo1"]], t["bq1"], t["bk1"], t["bv1"], t["bo1"],
                  t["w1T"], t["b1"], t["gamma"], t["beta"], t["w2T"], t["b2"],
                  [t["wq3"], t["wk3"], t["wv3"]], t["bq3"], t["bk3"], t["bv3"], out)
    r = run_bass_kernel_spmd(nc, [arrays], core_ids=[0])
    return r.results[0]["out"]
```
